# Optimizing a Trainium2 kernel written in Bass

```python
import numpy as np
import jax
import jax.numpy as jnp

def _softmax(x, axis=-1):
    return jax.nn.softmax(x, axis=axis)

def _gelu(x):
    return jax.nn.gelu(x, approximate=True)

def _silu(x):
    return jax.nn.silu(x)

def _sigmoid(x):
    return jax.nn.sigmoid(x)

def _layernorm(x, axis=-1, eps=1e-05):
    m = jnp.mean(x, axis=axis, keepdims=True)
    v = jnp.var(x, axis=axis, keepdims=True)
    return (x - m) / jnp.sqrt(v + eps)

def _scatter_add(tgt, idx, src, axis=0):
    return tgt.at[idx].add(src)

def _segment_sum(src, seg, n):
    return jax.ops.segment_sum(src, seg, n)
kernel_name = 'mk_recurrent_d1_jaxref_r8_037b91'

def setup_inputs(seed: int=0):
    np.random.seed(seed)
    _w = jnp.asarray

    def _L0_attn_setup():
        import jax, jax.numpy as jnp
        import numpy as np
        import math
        B, S, D = (4, 128, 128)
        H, DK = (16, 64)
        NUM_BUCKETS = 32
        MAX_DISTANCE = 128

        def _relative_position_bucket(relative_position, bidirectional=True, num_buckets=32, max_distance=128):
            relative_buckets = jnp.zeros_like(relative_position)
            if bidirectional:
                num_buckets //= 2
                relative_buckets = relative_buckets + (relative_position > 0).astype(jnp.int32) * num_buckets
                relative_position = jnp.abs(relative_position)
            else:
                relative_position = -jnp.minimum(relative_position, jnp.zeros_like(relative_position))
            max_exact = num_buckets // 2
            is_small = relative_position < max_exact
            rp_safe = jnp.maximum(relative_position, 1)
            rel_if_large = max_exact + (jnp.log(rp_safe.astype(jnp.float32) / max_exact) / math.log(max_distance / max_exact) * (num_buckets - max_exact)).astype(jnp.int32)
            rel_if_large = jnp.minimum(rel_if_large, num_buckets - 1)
            return relative_buckets + jnp.where(is_small, relative_position, rel_if_large)

        def compute_bias(rel_bias_emb, query_length, key_length):
            ctx = jnp.arange(query_length, dtype=jnp.int32)[:, None]
            mem = jnp.arange(key_length, dtype=jnp.int32)[None, :]
            rp = mem - ctx
            buckets = _relative_position_bucket(rp, bidirectional=True, num_buckets=NUM_BUCKETS, max_distance=MAX_DISTANCE)
            values = rel_bias_emb[buckets]
            return jnp.transpose(values, (2, 0, 1))[None]
        key = jax.random.key(seed)
        ks = jax.random.split(key, 6)
        s = 1.0 / math.sqrt(D)
        return {'hidden_states': jax.random.normal(ks[0], (B, S, D), jnp.float32), 'Wq': jax.random.normal(ks[1], (D, H * DK), jnp.float32) * s, 'Wk': jax.random.normal(ks[2], (D, H * DK), jnp.float32) * s, 'Wv': jax.random.normal(ks[3], (D, H * DK), jnp.float32) * s, 'Wo': jax.random.normal(ks[4], (H * DK, D), jnp.float32) * s, 'rel_bias_emb': jax.random.normal(ks[5], (NUM_BUCKETS, H), jnp.float32)}
    _L0_attn_in = _L0_attn_setup()

    def _L0_ffn_setup():
        import jax, jax.numpy as jnp
        import numpy as np
        D = 128
        H = 512
        O = 128
        E = 8
        K = 2
        key = jax.random.key(seed)
        ks = jax.random.split(key, 8)
        B, S = (2, 256)
        x = jax.random.normal(ks[0], (B, S, D), dtype=jnp.float32)
        s = 0.02
        Wr = jax.random.normal(ks[1], (D, E), dtype=jnp.float32) * s
        br = jnp.zeros((E,), dtype=jnp.float32)
        W1 = jax.random.normal(ks[2], (E, D, H), dtype=jnp.float32) * s
        b1 = jnp.zeros((E, H), dtype=jnp.float32)
        W2 = jax.random.normal(ks[3], (E, H, O), dtype=jnp.float32) * s
        b2 = jnp.zeros((E, O), dtype=jnp.float32)
        return {'x': x, 'Wr': Wr, 'br': br, 'W1': W1, 'b1': b1, 'W2': W2, 'b2': b2}
    _L0_ffn_in = _L0_ffn_setup()
    _d = {'L0_attn_hidden_states': _L0_attn_in['hidden_states'], 'L0_attn_Wq': _L0_attn_in['Wq'], 'L0_attn_Wk': _L0_attn_in['Wk'], 'L0_attn_Wv': _L0_attn_in['Wv'], 'L0_attn_Wo': _L0_attn_in['Wo'], 'L0_attn_rel_bias_emb': _L0_attn_in['rel_bias_emb'], 'L0_ffn_Wr': _L0_ffn_in['Wr'], 'L0_ffn_br': _L0_ffn_in['br'], 'L0_ffn_W1': _L0_ffn_in['W1'], 'L0_ffn_b1': _L0_ffn_in['b1'], 'L0_ffn_W2': _L0_ffn_in['W2'], 'L0_ffn_b2': _L0_ffn_in['b2']}
    _x0 = _d['L0_attn_hidden_states']
    _d['L0_attn_hidden_states'] = jax.random.normal(jax.random.fold_in(jax.random.key(seed), 1), (1, 2048, 128), dtype=_x0.dtype)
    del _x0
    return _d

def reference(L0_attn_hidden_states, L0_attn_Wq, L0_attn_Wk, L0_attn_Wv, L0_attn_Wo, L0_attn_rel_bias_emb, L0_ffn_Wr, L0_ffn_br, L0_ffn_W1, L0_ffn_b1, L0_ffn_W2, L0_ffn_b2):

    def _L0_attn_ref(hidden_states, Wq, Wk, Wv, Wo, rel_bias_emb):
        import jax, jax.numpy as jnp
        import numpy as np
        import math
        B, S, D = (4, 128, 128)
        H, DK = (16, 64)
        NUM_BUCKETS = 32
        MAX_DISTANCE = 128

        def _relative_position_bucket(relative_position, bidirectional=True, num_buckets=32, max_distance=128):
            relative_buckets = jnp.zeros_like(relative_position)
            if bidirectional:
                num_buckets //= 2
                relative_buckets = relative_buckets + (relative_position > 0).astype(jnp.int32) * num_buckets
                relative_position = jnp.abs(relative_position)
            else:
                relative_position = -jnp.minimum(relative_position, jnp.zeros_like(relative_position))
            max_exact = num_buckets // 2
            is_small = relative_position < max_exact
            rp_safe = jnp.maximum(relative_position, 1)
            rel_if_large = max_exact + (jnp.log(rp_safe.astype(jnp.float32) / max_exact) / math.log(max_distance / max_exact) * (num_buckets - max_exact)).astype(jnp.int32)
            rel_if_large = jnp.minimum(rel_if_large, num_buckets - 1)
            return relative_buckets + jnp.where(is_small, relative_position, rel_if_large)

        def compute_bias(rel_bias_emb, query_length, key_length):
            ctx = jnp.arange(query_length, dtype=jnp.int32)[:, None]
            mem = jnp.arange(key_length, dtype=jnp.int32)[None, :]
            rp = mem - ctx
            buckets = _relative_position_bucket(rp, bidirectional=True, num_buckets=NUM_BUCKETS, max_distance=MAX_DISTANCE)
            values = rel_bias_emb[buckets]
            return jnp.transpose(values, (2, 0, 1))[None]
        b, s, _ = hidden_states.shape

        def shape_heads(x):
            return x.reshape(b, s, H, DK).transpose(0, 2, 1, 3)
        q = shape_heads(hidden_states @ Wq)
        k = shape_heads(hidden_states @ Wk)
        v = shape_heads(hidden_states @ Wv)
        scores = jnp.einsum('bhqd,bhkd->bhqk', q, k)
        position_bias = compute_bias(rel_bias_emb, s, s)
        scores = scores + position_bias
        attn = jax.nn.softmax(scores.astype(jnp.float32), axis=-1).astype(scores.dtype)
        ctx = jnp.einsum('bhqk,bhkd->bhqd', attn, v)
        ctx = ctx.transpose(0, 2, 1, 3).reshape(b, s, H * DK)
        return ctx @ Wo

    def _L0_ffn_ref(x, Wr, br, W1, b1, W2, b2):
        import jax, jax.numpy as jnp
        import numpy as np
        D = 128
        H = 512
        O = 128
        E = 8
        K = 2
        B, S, _ = x.shape
        T = B * S
        xf = x.reshape(T, D)
        logits = xf @ Wr + br
        topk_logits, topk_idx = jax.lax.top_k(logits, K)
        gates = jax.nn.softmax(topk_logits, axis=1)
        dense_gates = jnp.zeros((T, E), dtype=logits.dtype).at[jnp.arange(T)[:, None], topk_idx].set(gates)
        h = jax.nn.relu(jnp.einsum('td,edh->teh', xf, W1) + b1)
        y = jnp.einsum('teh,eho->teo', h, W2) + b2
        out = jnp.einsum('te,teo->to', dense_gates, y)
        return out.reshape(B, S, O)
    x = L0_attn_hidden_states
    xn = _layernorm(x, axis=-1)
    s = _L0_attn_ref(xn, L0_attn_Wq, L0_attn_Wk, L0_attn_Wv, L0_attn_Wo, L0_attn_rel_bias_emb)
    g = _silu(_L0_ffn_ref(xn, L0_ffn_Wr, L0_ffn_br, L0_ffn_W1, L0_ffn_b1, L0_ffn_W2, L0_ffn_b2))
    x = x + s * g
    return x

_drawn_inputs = setup_inputs


def setup_inputs(seed=0):
    import zlib

    import numpy as np

    out = dict(_drawn_inputs(seed))
    spreads = {'L0_ffn_br': (0.0, 0.1), 'L0_ffn_b1': (0.0, 0.348), 'L0_ffn_b2': (0.0, 0.1)}
    factors = {'L0_attn_rel_bias_emb': 2.837}
    for name, (base, spread) in spreads.items():
        noise = np.random.default_rng([zlib.crc32(name.encode()), seed]).standard_normal(out[name].shape)
        drawn = base * np.exp(spread * noise) if base else spread * noise
        out[name] = jnp.asarray(drawn.astype(out[name].dtype))
    for name, factor in factors.items():
        out[name] = (out[name] * factor).astype(out[name].dtype)
    return out
```

```python
import concourse.bass as bass
from concourse import mybir
from contextlib import ExitStack

P = 128
S, D = 2048, 128
H, DK = 16, 64
NT = S // P
CH = 512
NC = S // CH
TC = CH // P
E, FF = 8, 512
NJ = FF // P
NPAIR = H // 2
NEAR = 3 * P
SAT = 91
BODY = 2 * NC
NUNIT = NPAIR * NC
NITER = NUNIT // BODY
RING = 8
EPS = 1e-5

F32, F32R, F16 = mybir.dt.float32, mybir.dt.float32r, mybir.dt.float16
ALU = mybir.AluOpType
ACT = mybir.ActivationFunctionType
AX = mybir.AxisListType.X


def need(eng, sem, value):
    if not isinstance(value, int) or value > 0:
        eng.wait_ge(sem, value)


def raw(ap):
    return ap.bitcast(F32)


def prepare(nc, x, emb, onehot, ident_c, wr, br, xh, xl, ident, vec, tabs, gates_d):
    with ExitStack() as ctx:
        t_ = lambda name, shape, dt=F32: ctx.enter_context(nc.sbuf_tensor(name, shape, dt))
        s_ = lambda name: ctx.enter_context(nc.semaphore(name))
        ps = [ctx.enter_context(nc.psum_tensor(f"pp{i}", [P, CH], F32)) for i in range(8)]
        xt, xn = t_("xt", [P, NT, D]), t_("xn", [P, NT, D])
        st, mv = t_("st", [P, NT, 6]), t_("mv", [P, NT, 2])
        va, sd, rs, t1, t2 = (t_(n, [P, NT]) for n in ("va", "sd", "rs", "t1", "t2"))
        emb_s, oh = t_("emb_s", [32, H]), t_("oh", [32, 2, CH])
        u_s = t_("u_s", [H, 2, CH])
        wr_s, wrh, wrl = t_("wr_s", [P, E]), t_("wrh", [P, E], F32R), t_("wrl", [P, E], F32R)
        br_s = t_("br_s", [P, E])
        lg, sel, cmp_, ex = (t_(n, [P, NT, E]) for n in ("lg", "sel", "cmp", "ex"))
        m1, z1 = t_("m1", [P, NT]), t_("z1", [P, NT])
        g8 = t_("g8", [E, S])
        s_x, s_c, s_o = s_("a_x"), s_("a_const"), s_("a_store")
        var_ready, sd_ready, xn_ready = s_("a_var"), s_("a_sd"), s_("a_xn")
        xt_ready, xh_ready, xl_ready = s_("a_xt"), s_("a_xh"), s_("a_xl")
        u_ready, u_saved, wr_ready = s_("a_u"), s_("a_usaved"), s_("a_wr")
        lg_ready, mm_ready, ex_ready, gate_ready = s_("a_lg"), s_("a_shift"), s_("a_ex"), s_("a_gate")
        g8_ready, g8_saved, chain = s_("a_g8"), s_("a_g8saved"), s_("a_chain")
        vec_done = s_("a_vec")
        with nc.Block() as block:
            @block.sync
            def _(sp):
                sp.dma_start(xt[:, :, :], x.rearrange("o (t p) d -> p (o t) d", p=P)).then_inc(s_x, 16)
                sp.dma_start(emb_s[:, :], emb).then_inc(s_c, 16)
                sp.dma_start(oh[:, :, :], onehot).then_inc(s_c, 16)
                sp.dma_start(ident[:, :], ident_c).then_inc(s_c, 16)
                sp.dma_start(wr_s[:, :], wr).then_inc(s_c, 16)
                sp.dma_start(br_s[:, :], br.partition_broadcast(P)).then_inc(s_c, 16)
                sp.wait_ge(u_saved, 2)
                sp.dma_start(vec.rearrange("a h n -> h a n"), u_s[:, :, :]).then_inc(vec_done, 16)
                sp.wait_ge(vec_done, 16)
                for a in range(2):
                    window = bass.AP(tensor=vec.tensor, offset=a * H * CH + P - 1,
                                     ap=[[CH, H], [-1, P], [1, NEAR]])
                    sp.dma_start(tabs[a], window).then_inc(s_o, 16)
                sp.wait_ge(g8_saved, NC)
                sp.dma_start(gates_d, g8[:, :]).then_inc(s_o, 16)
                sp.wait_ge(s_o, 48)

            @block.vector
            def _(dve):
                done = [0]

                def link(ins):
                    done[0] += 1
                    ins.then_inc(chain, 1)
                    dve.wait_ge(chain, done[0])

                dve.wait_ge(s_x, 16)
                for t in range(NT):
                    last = nc.vector.bn_stats(st[:, t, :], xt[:, t, :])
                link(last)
                for t in range(NT):
                    last = nc.vector.bn_aggr(mv[:, t, :], st[:, t, :])
                link(last)
                nc.vector.tensor_scalar(va[:, :], mv[:, :, 1], EPS, None, ALU.add).then_inc(var_ready, 1)
                dve.wait_ge(sd_ready, 1)
                link(nc.vector.reciprocal(rs[:, :], sd[:, :]))
                link(nc.vector.tensor_tensor(t1[:, :], rs[:, :], rs[:, :], ALU.mult))
                link(nc.vector.tensor_tensor(t2[:, :], t1[:, :], va[:, :], ALU.mult))
                link(nc.vector.tensor_scalar(t1[:, :], t2[:, :], -0.5, 1.5, ALU.mult, ALU.add))
                link(nc.vector.tensor_tensor(sd[:, :], rs[:, :], t1[:, :], ALU.mult))
                for t in range(NT):
                    nc.vector.tensor_scalar(xn[:, t, :], xt[:, t, :], mv[:, t, 0:1], sd[:, t:t + 1],
                                            ALU.subtract, ALU.mult).then_inc(xn_ready, 1)
                for c in range(NC):
                    dve.wait_ge(xh_ready, c + 1)
                    nc.vector.tensor_tensor(xl[:, c * CH:(c + 1) * CH], ps[c][:, :],
                                            raw(xh[:, c * CH:(c + 1) * CH]), ALU.subtract).then_inc(xl_ready, 1)
                dve.wait_ge(s_c, 80)
                link(nc.vector.tensor_copy(wrh[:, :], wr_s[:, :]))
                nc.vector.tensor_tensor(wrl[:, :], wr_s[:, :], raw(wrh[:, :]), ALU.subtract).then_inc(wr_ready, 1)
                dve.wait_ge(u_ready, 1)
                for a in range(2):
                    nc.vector.tensor_copy(u_s[:, a, :], ps[4 + a][0:H, :]).then_inc(u_saved, 1)
                dve.wait_ge(lg_ready, 1)
                link(nc.vector.tensor_tensor(lg[:, :, :], ps[6][:, 0:NT * E].rearrange("p (t e) -> p t e", e=E),
                                             br_s[:, :].unsqueeze(1).to_broadcast([P, NT, E]), ALU.add))
                link(nc.vector.reduce_max(m1[:, :], lg[:, :, :], AX))
                link(nc.vector.tensor_tensor(ex[:, :, :], lg[:, :, :],
                                             m1[:, :].unsqueeze(2).to_broadcast([P, NT, E]), ALU.subtract))
                nc.vector.memset(sel[:, :, :], 0.0).then_inc(mm_ready, 1)
                for o in range(E):
                    for lo, hi, op in ((0, o, ALU.is_gt), (o, E, ALU.is_ge)):
                        if hi > lo:
                            other = lg[:, :, o:o + 1].to_broadcast([P, NT, hi - lo])
                            last = nc.vector.tensor_tensor(cmp_[:, :, lo:hi], other, lg[:, :, lo:hi], op)
                    link(last)
                    link(nc.vector.tensor_tensor(sel[:, :, :], sel[:, :, :], cmp_[:, :, :], ALU.add))
                link(nc.vector.tensor_scalar(sel[:, :, :], sel[:, :, :], 2.5, None, ALU.is_lt))
                dve.wait_ge(ex_ready, 1)
                link(nc.vector.tensor_tensor(ex[:, :, :], ex[:, :, :], sel[:, :, :], ALU.mult))
                link(nc.vector.reduce_sum(z1[:, :], ex[:, :, :], AX))
                link(nc.vector.reciprocal(m1[:, :], z1[:, :]))
                nc.vector.tensor_tensor(sel[:, :, :], ex[:, :, :],
                                        m1[:, :].unsqueeze(2).to_broadcast([P, NT, E]), ALU.mult).then_inc(gate_ready, 1)
                for c in range(NC):
                    dve.wait_ge(g8_ready, c + 1)
                    nc.vector.tensor_copy(g8[:, c * CH:(c + 1) * CH], ps[c][0:E, :]).then_inc(g8_saved, 1)

            @block.scalar
            def _(act):
                act.wait_ge(var_ready, 1)
                nc.scalar.activation(sd[:, :], va[:, :], ACT.Sqrt).then_inc(sd_ready, 1)
                for c in range(NC):
                    act.wait_ge(xt_ready, c + 1)
                    nc.scalar.activation(xh[:, c * CH:(c + 1) * CH], ps[c][:, :], ACT.Copy).then_inc(xh_ready, 1)
                act.wait_ge(mm_ready, 1)
                nc.scalar.activation(ex[:, :, :], ex[:, :, :], ACT.Exp).then_inc(ex_ready, 1)

            @block.tensor
            def _(pe):
                pe.wait_ge(s_c, 80)
                for a in range(2):
                    last = nc.tensor.matmul(ps[4 + a][0:H, :], emb_s[:, :], oh[:, a, :], start=True, stop=True)
                last.then_inc(u_ready, 1)
                for c in range(NC):
                    pe.wait_ge(xn_ready, (c + 1) * TC)
                    for i in range(TC):
                        last = nc.tensor.transpose(ps[c][:, i * P:(i + 1) * P], xn[:, c * TC + i, :], ident[:, :])
                    last.then_inc(xt_ready, 1)
                pe.wait_ge(wr_ready, 1)
                for t in range(NT):
                    pe.wait_ge(xl_ready, t // TC + 1)
                    out = ps[6][:, t * E:(t + 1) * E]
                    parts = [(a, b) for a in (xh, xl) for b in (wrh, wrl)]
                    for n, (a, b) in enumerate(parts):
                        last = nc.tensor.matmul(out, a[:, t * P:(t + 1) * P], b[:, :], start=n == 0, stop=n == 3)
                last.then_inc(lg_ready, 1)
                pe.wait_ge(gate_ready, 1)
                for c in range(NC):
                    for i in range(TC):
                        last = nc.tensor.transpose(ps[c][0:E, i * P:(i + 1) * P], sel[:, c * TC + i, :], ident[:, :])
                    last.then_inc(g8_ready, 1)


def experts(nc, w1, b1, w2, b2, xh, xl, gates_d, silu_d):
    with ExitStack() as ctx:
        t_ = lambda name, shape, dt=F32: ctx.enter_context(nc.sbuf_tensor(name, shape, dt))
        s_ = lambda name: ctx.enter_context(nc.semaphore(name))
        hp = [ctx.enter_context(nc.psum_tensor(f"hp{i}", [P, CH], F32)) for i in range(NJ)]
        yp = [ctx.enter_context(nc.psum_tensor(f"yp{i}", [P, CH], F32)) for i in range(2)]
        w1r, w2r = t_("w1r", [P, 2, FF]), t_("w2r", [P, 2, NJ, D])
        w1h, w1l = t_("w1h", [P, 2, FF], F32R), t_("w1l", [P, 2, FF], F32R)
        w2h, w2l = t_("w2h", [P, 2, NJ * D], F32R), t_("w2l", [P, 2, NJ * D], F32R)
        b1s, b2s = t_("b1s", [P, 2, NJ]), t_("b2s", [P, 2, 1])
        gb = t_("gb", [P, 2, S])
        h32 = t_("h32", [P, 2, NJ, CH])
        hh, hl = t_("hh", [P, 2, NJ, CH], F32R), t_("hl", [P, 2, NJ, CH], F32R)
        yg = t_("yg", [P, 2, CH])
        fT = t_("fT", [P, S])
        en = t_("en", [P, S])
        loaded = [s_("f_loaded0"), s_("f_loaded1")]
        hi_split, split, stored = s_("f_hi_split"), s_("f_split"), s_("f_stored")
        gload = [s_("f_gload0"), s_("f_gload1")]
        hp_ready, h32_ready, h_ready, yp_ready = s_("f_hp"), s_("f_h32"), s_("f_h"), s_("f_yp")
        hh_ready, yg_ready, sum_done = s_("f_hh"), s_("f_yg"), s_("f_sum")
        e_ready, one_ready, silu_ready = s_("f_e"), s_("f_one"), s_("f_silu")
        bodies = 2 * NC

        def loop(eng, body):
            body(0, True, False)
            with eng.Fori(1, E // 2 - 1) as it:
                body(it, False, False)
            body(E // 2 - 1, False, True)

        with nc.Block() as block:
            @block.sync
            def _(sp):
                def body(it, first, last):
                    for b in range(2):
                        e = it * 2 + b
                        need(sp, yg_ready, (e - 1) * NC)
                        sp.dma_start(w1r[:, b, :], w1[bass.ds(e, 1), :, :].rearrange("e d h -> d (e h)")).then_inc(loaded[b], 16)
                        sp.dma_start(w2r[:, b, :, :], w2[bass.ds(e, 1), :, :].rearrange("e (j p) o -> p (e j) o", p=P)).then_inc(loaded[b], 16)
                        sp.dma_start(b1s[:, b, :], b1[bass.ds(e, 1), :].rearrange("e (j p) -> p (e j)", p=P), allow_slow_non_contiguous=True).then_inc(loaded[b], 16)
                        sp.dma_start(b2s[:, b, :], b2[bass.ds(e, 1), :].rearrange("e p -> p e"), allow_slow_non_contiguous=True).then_inc(loaded[b], 16)
                        g = bass.AP(tensor=gates_d.tensor, offset=e * S, ap=[[0, P], [1, S]])
                        sp.dma_start(gb[:, b, :], g).then_inc(gload[b], 16)
                loop(sp, body)
                sp.wait_ge(silu_ready, NC)
                sp.dma_start(silu_d, fT[:, :]).then_inc(stored, 16)
                sp.wait_ge(stored, 16)

            @block.gpsimd
            def _(pool):
                nc.gpsimd.memset(fT[:, :], 0.0).then_inc(sum_done, 1)

                def add(n, c):
                    pool.wait_ge(yg_ready, n + 1)
                    pool.wait_ge(sum_done, n + 1)
                    nc.gpsimd.tensor_tensor(fT[:, c * CH:(c + 1) * CH], fT[:, c * CH:(c + 1) * CH],
                                            yg[:, c % 2, :], ALU.add).then_inc(sum_done, 1)

                def body(it, first, last):
                    for b in range(2):
                        e = it * 2 + b
                        need(pool, yp_ready, (e - 1) * NC)
                        w2f = w2r[:, b, :, :].rearrange("p j o -> p (j o)")
                        pool.wait_ge(hi_split, e * 2 + 2)
                        nc.gpsimd.tensor_tensor(w1l[:, b, :], w1r[:, b, :], raw(w1h[:, b, :]), ALU.subtract).then_inc(split, 1)
                        nc.gpsimd.tensor_tensor(w2l[:, b, :], w2f, raw(w2h[:, b, :]), ALU.subtract).then_inc(split, 1)
                        for c in range(NC):
                            if not (first and b == 0):
                                add((e - 1) * NC + c, c)
                loop(pool, body)
                for c in range(NC):
                    add((E - 1) * NC + c, c)

            @block.tensor
            def _(pe):
                def up(it, b, c):
                    e = it * 2 + b
                    n = e * NC + c
                    if c == 0:
                        pe.wait_ge(split, e * 2 + 2)
                    for j in range(NJ):
                        need(pe, h32_ready, (n - 1) * NJ + j + 1)
                        w = slice(j * P, (j + 1) * P)
                        xs = slice(c * CH, (c + 1) * CH)
                        nc.tensor.matmul(hp[j][:, :], w1h[:, b, w], xh[:, xs], start=True, stop=False)
                        nc.tensor.matmul(hp[j][:, :], w1l[:, b, w], xh[:, xs], start=False, stop=False)
                        nc.tensor.matmul(hp[j][:, :], w1h[:, b, w], xl[:, xs], start=False, stop=True).then_inc(hp_ready, 1)

                def down(it, b, c):
                    n = (it * 2 + b) * NC + c
                    need(pe, yg_ready, n - 1)
                    for j in range(NJ):
                        pe.wait_ge(h_ready, n * NJ + j + 1)
                        w = slice(j * P, (j + 1) * P)
                        nc.tensor.matmul(yp[c % 2][:, :], w2h[:, b, w], hh[:, c % 2, j, :], start=j == 0, stop=False)
                        nc.tensor.matmul(yp[c % 2][:, :], w2l[:, b, w], hh[:, c % 2, j, :], start=False, stop=False)
                        last = nc.tensor.matmul(yp[c % 2][:, :], w2h[:, b, w], hl[:, c % 2, j, :], start=False, stop=j == NJ - 1)
                    last.then_inc(yp_ready, 1)

                def body(it, first, last):
                    for b in range(2):
                        for c in range(NC):
                            up(it, b, c)
                            if c:
                                down(it, b, c - 1)
                            elif b:
                                down(it, 0, NC - 1)
                            elif not first:
                                down(it - 1, 1, NC - 1)
                loop(pe, body)
                down(E // 2 - 1, 1, NC - 1)

            @block.scalar
            def _(act):
                def split_high(it, b):
                    act.wait_ge(loaded[b], (it + 1) * 64)
                    need(act, yp_ready, (it * 2 + b - 1) * NC)
                    nc.scalar.activation(w1h[:, b, :], w1r[:, b, :], ACT.Copy).then_inc(hi_split, 1)
                    nc.scalar.activation(w2h[:, b, :], w2r[:, b, :, :].rearrange("p j o -> p (j o)"),
                                         ACT.Copy).then_inc(hi_split, 1)

                split_high(0, 0)

                def body(it, first, last):
                    for b in range(2):
                        e = it * 2 + b
                        for c in range(NC):
                            if c == 2 and not (last and b):
                                split_high(it + b, 1 - b)
                            n = e * NC + c
                            for j in range(NJ):
                                act.wait_ge(hp_ready, n * NJ + j + 1)
                                need(act, h_ready, (n - 2) * NJ + j + 1)
                                nc.scalar.activation(h32[:, c % 2, j, :], hp[j][:, :], ACT.Relu,
                                                     bias=b1s[:, b, j:j + 1]).then_inc(h32_ready, 1)
                loop(act, body)
                for c in range(NC):
                    act.wait_ge(sum_done, E * NC - NC + c + 2)
                    nc.scalar.activation(en[:, c * CH:(c + 1) * CH], fT[:, c * CH:(c + 1) * CH], ACT.Exp,
                                         scale=-1.0).then_inc(e_ready, 1)

            @block.vector
            def _(dve):
                def halves(it, b, c):
                    n = (it * 2 + b) * NC + c
                    for j in range(NJ):
                        dve.wait_ge(h32_ready, n * NJ + j + 1)
                        if j == 0:
                            need(dve, yp_ready, n - 1)
                        nc.vector.tensor_copy(hh[:, c % 2, j, :], h32[:, c % 2, j, :]).then_inc(hh_ready, 1)
                        dve.wait_ge(hh_ready, n * NJ + j + 1)
                        nc.vector.tensor_tensor(hl[:, c % 2, j, :], h32[:, c % 2, j, :],
                                                raw(hh[:, c % 2, j, :]), ALU.subtract).then_inc(h_ready, 1)

                def gated(it, b, c):
                    e = it * 2 + b
                    n = e * NC + c
                    if c == 0:
                        dve.wait_ge(gload[b], (it + 1) * 16)
                        dve.wait_ge(loaded[b], (it + 1) * 64)
                    dve.wait_ge(yp_ready, n + 1)
                    need(dve, sum_done, n)
                    nc.vector.scalar_tensor_tensor(out=yg[:, c % 2, :], in0=yp[c % 2][:, :], scalar=b2s[:, b, 0:1],
                                                   in1=gb[:, b, c * CH:(c + 1) * CH], op0=ALU.add,
                                                   op1=ALU.mult).then_inc(yg_ready, 1)

                def body(it, first, last):
                    for b in range(2):
                        for c in range(NC):
                            halves(it, b, c)
                            if c:
                                gated(it, b, c - 1)
                            elif b:
                                gated(it, 0, NC - 1)
                            elif not first:
                                gated(it - 1, 1, NC - 1)
                loop(dve, body)
                gated(E // 2 - 1, 1, NC - 1)
                for c in range(NC):
                    cs = slice(c * CH, (c + 1) * CH)
                    dve.wait_ge(e_ready, c + 1)
                    nc.vector.tensor_scalar(en[:, cs], en[:, cs], 1.0, None, ALU.add).then_inc(one_ready, 1)
                    dve.wait_ge(one_ready, 2 * c + 1)
                    nc.vector.reciprocal(en[:, cs], en[:, cs]).then_inc(one_ready, 1)
                    dve.wait_ge(one_ready, 2 * c + 2)
                    nc.vector.tensor_tensor(fT[:, cs], fT[:, cs], en[:, cs], ALU.mult).then_inc(silu_ready, 1)


def near_columns(r):
    start = (r - 1) * P
    lo = max(start if r <= 1 else start + P - SAT + 1, 0)
    hi = min(start + 2 * P + SAT - 1 if r <= 1 else start + NEAR, CH)
    return slice(lo, hi), slice(lo - start, hi - start)


def chunks_of(s):
    return [5 * s // 2 + i for i in range(5 * (s + 1) // 2 - 5 * s // 2) if 5 * s // 2 + i < 2 * TC * NC]


def attention(nc, wq, wk, wv, wo, tabs, mask_c, xh, xl, ident, sT):
    with ExitStack() as ctx:
        t_ = lambda name, shape, dt=F32: ctx.enter_context(nc.sbuf_tensor(name, shape, dt))
        s_ = lambda name: ctx.enter_context(nc.semaphore(name))
        bank = lambda name: ctx.enter_context(nc.psum_tensor(name, [P, CH], F32))
        SM = [bank("SM0"), bank("SM1")]
        ST = [bank("ST0"), bank("ST1")]
        CT = [bank("CT0"), bank("CT1")]
        MV = bank("MV")
        MP = bank("MP")
        Q1 = [t_(f"Q1{h}", [P, S], F32R) for h in range(2)]
        Q2 = [t_(f"Q2{h}", [P, S], F32R) for h in range(2)]
        K1 = [[t_(f"K1{b}{h}", [P, S], F32R) for h in range(2)] for b in range(2)]
        K2 = [[t_(f"K2{b}{h}", [P, S], F32R) for h in range(2)] for b in range(2)]
        V = [t_(f"V{b}", [P, NT, 2 * DK]) for b in range(2)]
        PR = t_("PR", [P, RING, CH])
        Z = t_("Z", [P, 2, 2, CH])
        rz = t_("rz", [P, CH])
        TR = t_("TR", [P, 2, NEAR])
        TH = t_("TH", [P, 2, 2, 2, NEAR], F32R)
        TL = t_("TL", [P, 2, 2, 2, NEAR], F16)
        TM = t_("TM", [P, 2, 2, 2, NEAR], F32R)
        far = t_("far", [P, 2, 2, 2])
        fd = t_("fd", [P, 2])
        fm = t_("fm", [P, 2, 2, NT, NC])
        WR, WH, WL = t_("WR", [P, 3 * P]), t_("WH", [P, 2, 3 * P], F32R), t_("WL", [P, 2, 3 * P], F32R)
        WO = t_("WO", [P, 2, D])
        identr, ident16 = t_("identr", [P, P], F32R), t_("ident16", [P, P], F16)
        ones = t_("ones", [P, DK])
        mask = t_("mask", [P, NT, NC])
        mx, mxb, nm = t_("mx", [P, 2, TC, NC]), t_("mxb", [P, 2, TC, NC]), t_("nm", [P, 2, TC])

        w_loaded, t_loaded, c_loaded = s_("w_loaded"), s_("t_loaded"), s_("c_loaded")
        wo_loaded = [s_("wo_loaded0"), s_("wo_loaded1")]
        q_copied = [s_("q_copied0"), s_("q_copied1")]
        k_copied = [s_("k_copied0"), s_("k_copied1")]
        const_ready, wh_ready, wl_ready, tab_ready = s_("const_ready"), s_("wh_ready"), s_("wl_ready"), s_("tab_ready")
        mp_ready, hi_ready, mp_free = s_("mp_ready"), s_("hi_ready"), s_("mp_free")
        sm_ready, mx_ready, nm_ready = s_("sm_ready"), s_("mx_ready"), s_("nm_ready")
        mt_ready, rows_ready = s_("mt_ready"), s_("rows_ready")
        st_ready, exp_ready, pv_done, z_done = s_("st_ready"), s_("exp_ready"), s_("pv_done"), s_("z_done")
        zb_ready, ctx_ready, wo_ready, sum_ready = s_("zb_ready"), s_("ctx_ready"), s_("wo_ready"), s_("sum_ready")
        chain = s_("dve_chain")

        job_list = {0: [("q", 12, 0)],
                    1: [("k", 3, 0), ("v", 5, 0), ("k", 7, 1), ("v", 9, 1), ("q", 12, 0)],
                    2: [("k", 3, 2), ("v", 5, 2), ("k", 7, 3), ("v", 9, 3), ("q", 12, 0)],
                    3: [("q", 12, 0)]}
        start_jobs = [("k", c) for c in range(4)] + [("v", c) for c in range(4)] + [("q", 0), ("q", 1)]

        def jobs_before(l):
            full = [k for m in range(l) for k, _, _ in job_list[m % NC]]
            return len(full), sum(k != "v" for k in full)

        JOBS, HIGHS = jobs_before(BODY)

        def jobs(it, l, last):
            n, m = jobs_before(l)
            n, m = n + 10 + it * JOBS, m + 6 + it * HIGHS
            out = []
            for kind, slot, c in job_list[l % NC]:
                if last and (l >= NC and kind != "q" or l + 2 >= BODY):
                    continue
                out.append((kind, slot, c, n, m))
                n, m = n + 1, m + (kind != "v")
            return out

        def loop(eng, body):
            body(0, True, False)
            with eng.Fori(1, NITER - 1) as it:
                body(it, False, False)
            body(NITER - 1, False, True)

        with nc.Block() as block:
            @block.sync
            def _(sp):
                sp.dma_start(mask[:, :, :], mask_c).then_inc(c_loaded, 16)

                def weights(p):
                    cols = bass.ds(p * P, P)
                    for n, w in enumerate((wq, wk, wv)):
                        sp.dma_start(WR[:, n * P:(n + 1) * P], w[:, cols]).then_inc(w_loaded, 16)

                def table(p, h):
                    for a in range(2):
                        sp.dma_start(TR[:, a, :], tabs[a][bass.ds(p * 2 + h, 1), :, :].rearrange("h p n -> p (h n)")
                                     ).then_inc(t_loaded, 16)

                def load_wo(p, b):
                    sp.dma_start(WO[:, b, :], wo[bass.ds(p * P, P), :]).then_inc(wo_loaded[b], 16)

                def copy_q(u, m):
                    sp.wait_ge(hi_ready, m + 1)
                    for h in range(2):
                        cs = slice(u * CH, (u + 1) * CH)
                        sp.dma_start(raw(Q1[h][DK:P, cs]), raw(Q1[h][0:DK, cs])).then_inc(q_copied[u % 2], 16)

                def copy_k(b, c, m):
                    sp.wait_ge(hi_ready, m + 1)
                    for h in range(2):
                        cs = slice(c * CH, (c + 1) * CH)
                        sp.dma_start(raw(K2[b][h][0:DK, cs]), raw(K1[b][h][0:DK, cs])).then_inc(k_copied[b], 16)

                weights(0)
                table(0, 0)
                load_wo(0, 0)
                sp.wait_ge(tab_ready, 1)
                table(0, 1)
                for c in range(NC):
                    copy_k(0, c, c)
                for u in range(2):
                    copy_q(u, NC + u)

                def body(it, first, last):
                    for l in range(BODY):
                        b, u = l // NC, l % NC
                        p = it * 2 + b
                        more = not (last and b)
                        if u == 0 and more:
                            sp.wait_ge(wl_ready, p + 1)
                            weights(p + 1)
                            sp.wait_ge(tab_ready, p * 2 + 2)
                            table(p + 1, 0)
                        if u == 1 and more:
                            sp.wait_ge(wo_ready, it * BODY + l - 1)
                            load_wo(p + 1, 1 - b)
                        if u == 2 and more:
                            sp.wait_ge(tab_ready, p * 2 + 3)
                            table(p + 1, 1)
                        for kind, _, c, _, m in jobs(it, l, last):
                            if kind == "k":
                                copy_k(1 - b, c, m)
                            elif kind == "q":
                                copy_q((u + 2) % NC, m)
                loop(sp, body)

            @block.gpsimd
            def _(pool):
                nc.gpsimd.memset(sT[:, :], 0.0).then_inc(const_ready, 1)
                pool.wait_ge(const_ready, 1)
                nc.gpsimd.memset(ones[:, :], 1.0).then_inc(const_ready, 1)
                for b in range(2):
                    for h in range(2):
                        pool.wait_ge(const_ready, 2 + 2 * b + h)
                        nc.gpsimd.memset(raw(K2[b][h][DK:DK + TC, :]), 1.0).then_inc(const_ready, 1)

                def body(it, first, last):
                    for l in range(BODY):
                        g = it * BODY + l
                        z = Z[:, l % 2, :, :]
                        tile = lambda k: PR[:, 2 * k % RING:2 * k % RING + 2, :]
                        for s in range(1, NT):
                            pool.wait_ge(exp_ready, g * 2 * NT + 2 * s + 2)
                            if s == 1:
                                need(pool, zb_ready, g - 1)
                                a = tile(0)
                            else:
                                pool.wait_ge(z_done, g * (NT - 1) + s - 1)
                                a = z
                            nc.gpsimd.tensor_tensor(z, a, tile(s), ALU.add).then_inc(z_done, 1)
                loop(pool, body)

            @block.tensor
            def _(pe):
                def split_product(out, a, b, first=True, last=True):
                    nc.tensor.matmul(out, a[0], b[0], start=first, stop=False)
                    nc.tensor.matmul(out, a[1], b[0], start=False, stop=False)
                    return nc.tensor.matmul(out, a[0], b[1], start=False, stop=last)

                def project(kind, b, c, n):
                    need(pe, mp_free, n)
                    if kind == "v":
                        w = slice(2 * P, 3 * P)
                        for i in range(TC):
                            xs = slice((c * TC + i) * P, (c * TC + i + 1) * P)
                            last = split_product(MP[:, i * P:(i + 1) * P], (xh[:, xs], xl[:, xs]),
                                                 (WH[:, b, w], WL[:, b, w]))
                    else:
                        w = slice(0, P) if kind == "q" else slice(P, 2 * P)
                        xs = slice(c * CH, (c + 1) * CH)
                        last = split_product(MP[:, :], (WH[:, b, w], WL[:, b, w]), (xh[:, xs], xl[:, xs]))
                    last.then_inc(mp_ready, 1)

                def maxima(n0, b, u, m):
                    h, t, c = m // (TC * NC), m // NC % TC, m % NC
                    need(pe, mx_ready, n0 + m - 1)
                    T = u * TC + t
                    out = SM[m % 2]
                    r = T - c * TC
                    near = -1 <= r <= TC
                    last = nc.tensor.matmul(out[:, :], Q1[h][:, T * P:(T + 1) * P], K1[b][h][:, c * CH:(c + 1) * CH],
                                            start=True, stop=not near)
                    if near:
                        cols, of_table = near_columns(r)
                        last = nc.tensor.matmul(out[:, cols], identr[:, :], TM[:, b, h, int(r <= 1), of_table],
                                                start=False, stop=True)
                    last.then_inc(sm_ready, 1)

                def ready_for_maxima(p, u, g, n_job):
                    pe.wait_ge(mp_free, n_job + 1)
                    pe.wait_ge(q_copied[u % 2], (p * 2 + u // 2 + 1) * 32)
                    if u == 0:
                        pe.wait_ge(tab_ready, p * 2 + 2)

                def turn(g):
                    pe.wait_ge(nm_ready, g + 1)
                    need(pe, sum_ready, g - 1)
                    for h in range(2):
                        last = nc.tensor.transpose(MV[0:TC, h * P:(h + 1) * P], nm[:, h, :], ident[:, :])
                    last.then_inc(mt_ready, 1)

                def scores(g, b, u, s, h):
                    need(pe, exp_ready, g * 2 * NT + 2 * s + h - 1)
                    ks, qs = slice(s * P, (s + 1) * P), slice(u * CH, (u + 1) * CH)
                    r = s - u * TC
                    near = -1 <= r <= TC
                    nc.tensor.matmul(ST[h][:, :], K1[b][h][:, ks], Q1[h][:, qs], start=True, stop=False)
                    last = nc.tensor.matmul(ST[h][:, :], K2[b][h][0:DK + TC, ks], Q2[h][0:DK + TC, qs],
                                            start=False, stop=not near)
                    if near:
                        side, (cols, of_table) = int(r > 1), near_columns(r)
                        nc.tensor.matmul(ST[h][:, cols], identr[:, :], TH[:, b, h, side, of_table],
                                         start=False, stop=False)
                        last = nc.tensor.matmul(ST[h][:, cols], ident16[:, :], TL[:, b, h, side, of_table],
                                                start=False, stop=True)
                    last.then_inc(st_ready, 1)

                def values(g, b, par, s):
                    pe.wait_ge(exp_ready, g * 2 * NT + 2 * s + 2)
                    if s == 0:
                        need(pe, ctx_ready, g - 1)
                    for h in range(2):
                        rows = slice(h * DK, (h + 1) * DK)
                        last = nc.tensor.matmul(CT[par][rows, :], V[b][:, s, rows], PR[:, (2 * s + h) % RING, :],
                                                start=s == 0, stop=s == NT - 1)
                    last.then_inc(pv_done, 1)

                def sums(g, par):
                    pe.wait_ge(z_done, (g + 1) * (NT - 1))
                    pe.wait_ge(rows_ready, g + 1)
                    for h in range(2):
                        last = nc.tensor.matmul(MV[h * DK:(h + 1) * DK, :], ones[:, :], Z[:, par, h, :],
                                                start=True, stop=True)
                    last.then_inc(zb_ready, 1)

                def output(g, b, it):
                    pe.wait_ge(ctx_ready, g + 1)
                    pe.wait_ge(wo_loaded[b], (it + 1) * 16)
                    nc.tensor.matmul(MV[:, :], WO[:, b, :], rz[:, :], start=True, stop=True).then_inc(wo_ready, 1)

                pe.wait_ge(wl_ready, 1)
                for n, (kind, c) in enumerate(start_jobs):
                    project(kind, 0, c, n)
                ready_for_maxima(0, 0, 0, 8)
                for m in range(2 * TC * NC):
                    maxima(0, 0, 0, m)
                turn(0)

                def body(it, first, last):
                    for l in range(BODY):
                        b, u = l // NC, l % NC
                        g, p = it * BODY + l, it * 2 + b
                        nb, nu = (l + 1) % BODY // NC, (l + 1) % NC
                        lb, lit = ((l - 1) % BODY) // NC, it if l else it - 1
                        final = last and l == BODY - 1
                        todo = {slot: (kind, c, n) for kind, slot, c, n, _ in jobs(it, l, last)}
                        pe.wait_ge(rows_ready, g + 1)
                        if u == 0:
                            pe.wait_ge(k_copied[b], (it + 1) * 32 * NC)
                        if not final:
                            q_job = jobs(it, l - 1, last)[-1][3] if l else 9 + it * JOBS
                            ready_for_maxima(it * 2 + (l + 1) // NC, nu, g + 1, q_job)
                        for s in range(NT):
                            chunks = [] if final else chunks_of(s)
                            for h in range(2):
                                scores(g, b, u, s, h)
                                if h < len(chunks):
                                    maxima((g + 1) * 2 * TC * NC, nb, nu, chunks[h])
                            if s:
                                values(g, b, l % 2, s - 1)
                            elif not (first and l == 0):
                                values(g - 1, lb, (l - 1) % 2, NT - 1)
                            for m in chunks[2:]:
                                maxima((g + 1) * 2 * TC * NC, nb, nu, m)
                            if s == 14 and not final:
                                turn(g + 1)
                            if not (first and l == 0):
                                if s == 2:
                                    sums(g - 1, (l - 1) % 2)
                                if s == 8:
                                    output(g - 1, lb, lit)
                            if s in todo:
                                kind, c, n = todo[s]
                                if kind == "q":
                                    project("q", (l + 2) % BODY // NC, (u + 2) % NC, n)
                                else:
                                    project(kind, 1 - b, c, n)
                loop(pe, body)
                values(NUNIT - 1, 1, 1, NT - 1)
                pe.wait_ge(sum_ready, NUNIT - 1)
                sums(NUNIT - 1, 1)
                output(NUNIT - 1, 1, NITER - 1)

            @block.scalar
            def _(act):
                def split_weights(p, b):
                    act.wait_ge(w_loaded, (p + 1) * 48)
                    nc.scalar.activation(WH[:, b, :], WR[:, :], ACT.Copy).then_inc(wh_ready, 1)

                def high(kind, b, c, n):
                    act.wait_ge(mp_ready, n + 1)
                    for h in range(2):
                        dst = Q1[h] if kind == "q" else K1[b][h]
                        last = nc.scalar.activation(dst[0:DK, c * CH:(c + 1) * CH], MP[h * DK:(h + 1) * DK, :], ACT.Copy)
                    last.then_inc(hi_ready, 1)

                split_weights(0, 0)
                for n, (kind, c) in enumerate(start_jobs):
                    if kind != "v":
                        high(kind, 0, c, n)

                def body(it, first, last):
                    for l in range(BODY):
                        b, u = l // NC, l % NC
                        g, p = it * BODY + l, it * 2 + b
                        todo = {slot: (kind, c, n) for kind, slot, c, n, _ in jobs(it, l, last)}
                        if u == 0:
                            act.wait_ge(tab_ready, p * 2 + 2)
                        for s in range(NT):
                            for h in range(2):
                                n = g * 2 * NT + 2 * s + h
                                act.wait_ge(st_ready, n + 1)
                                if s >= 4 or not (first and l == 0):
                                    act.wait_ge(pv_done, g * NT + s - 3)
                                    if s >= 4:
                                        k = g * (NT - 1) + max(s - 5, 0) + 1
                                    else:
                                        k = (g - 1) * (NT - 1) + NT + s - 4
                                    act.wait_ge(z_done, k)
                                side = int(s - u * TC > 1)
                                nc.scalar.activation(PR[:, (2 * s + h) % RING, :], ST[h][:, :], ACT.Exp,
                                                     bias=far[:, b, h, side:side + 1]).then_inc(exp_ready, 1)
                            if s in todo and todo[s][0] != "v":
                                kind, c, n = todo[s]
                                high(kind, 1 - b, (u + 2) % NC if kind == "q" else c, n)
                            if s == 9 and u == 0 and not (last and b):
                                split_weights(p + 1, 1 - b)
                loop(act, body)

            @block.vector
            def _(dve):
                links = [0, None]

                def link(ins):
                    links[0] += 1
                    ins.then_inc(chain, 1)
                    dve.wait_ge(chain, links[0] if links[1] is None else links[1] + links[0])

                def split_weights(p, b):
                    dve.wait_ge(wh_ready, p + 1)
                    nc.vector.tensor_tensor(WL[:, b, :], WR[:, :], raw(WH[:, b, :]), ALU.subtract).then_inc(wl_ready, 1)

                def table_far(p, b, h):
                    dve.wait_ge(t_loaded, (p * 2 + h + 1) * 32)
                    nc.vector.tensor_copy(far[:, b, h, 0:1], TR[:, 0, NEAR - 1:NEAR])
                    link(nc.vector.tensor_copy(far[:, b, h, 1:2], TR[:, 0, 0:1]))
                    link(nc.vector.tensor_tensor(fd[:, h:h + 1], far[:, b, h, 1:2], far[:, b, h, 0:1], ALU.subtract))
                    dve.wait_ge(c_loaded, 16)
                    nc.vector.tensor_scalar(fm[:, b, h, :, :], mask[:, :, :], fd[:, h:h + 1], far[:, b, h, 0:1],
                                            ALU.mult, ALU.add)

                def table_side(b, h, side):
                    f = far[:, b, h, side:side + 1]
                    nc.vector.tensor_scalar(TM[:, b, h, side, :], TR[:, 1, :], f, None, ALU.subtract)
                    link(nc.vector.tensor_scalar(TH[:, b, h, side, :], TR[:, 0, :], f, None, ALU.subtract))
                    last = nc.vector.scalar_tensor_tensor(out=TL[:, b, h, side, :], in0=TR[:, 0, :], scalar=f,
                                                          in1=raw(TH[:, b, h, side, :]), op0=ALU.subtract,
                                                          op1=ALU.subtract)
                    if side:
                        last.then_inc(tab_ready, 1)

                def low(kind, b, c, n, m):
                    dve.wait_ge(mp_ready, n + 1)
                    if kind == "v":
                        nc.vector.tensor_copy(V[b][:, c * TC:(c + 1) * TC, :],
                                              MP[:, :].rearrange("p (t d) -> p t d", t=TC)).then_inc(mp_free, 1)
                        return
                    dve.wait_ge(hi_ready, m + 1)
                    for h in range(2):
                        cs = slice(c * CH, (c + 1) * CH)
                        src, hi = (Q2[h][0:DK, cs], Q1[h]) if kind == "q" else (K1[b][h][DK:P, cs], K1[b][h])
                        last = nc.vector.tensor_tensor(src, MP[h * DK:(h + 1) * DK, :], raw(hi[0:DK, cs]), ALU.subtract)
                    last.then_inc(mp_free, 1)

                def reduce(n0, m):
                    h, t, c = m // (TC * NC), m // NC % TC, m % NC
                    dve.wait_ge(sm_ready, n0 + m + 1)
                    nc.vector.reduce_max(mx[:, h, t, c:c + 1], SM[m % 2][:, :], AX).then_inc(mx_ready, 1)

                def combine(g, b, u):
                    dve.wait_ge(mx_ready, (g + 1) * 2 * TC * NC)
                    link(nc.vector.tensor_tensor(mxb[:, :, :, :], mx[:, :, :, :], fm[:, b, :, u * TC:(u + 1) * TC, :], ALU.add))
                    nc.vector.tensor_reduce(nm[:, :, :], mxb[:, :, :, :], AX, ALU.max, negate=True).then_inc(nm_ready, 1)

                def rows(g, u):
                    dve.wait_ge(mt_ready, g + 1)
                    for h in range(2):
                        src = MV[0:TC, h * P:(h + 1) * P].unsqueeze(1).to_broadcast([TC, TC, P])
                        dst = Q2[h][DK:DK + TC, u * CH:(u + 1) * CH].rearrange("p (t q) -> p t q", t=TC)
                        own = ident[0:TC, 0:TC].unsqueeze(2).to_broadcast([TC, TC, P])
                        last = nc.vector.tensor_tensor(dst, src, own, ALU.mult)
                    last.then_inc(rows_ready, 1)

                def invert(g, i):
                    if i == 0:
                        dve.wait_ge(zb_ready, g + 1)
                        need(dve, wo_ready, g)
                    cs = slice(i * P, (i + 1) * P)
                    ins = nc.vector.reciprocal(rz[:, cs], MV[:, cs])
                    return ins

                def normalise(g, par):
                    dve.wait_ge(pv_done, (g + 1) * NT)
                    nc.vector.tensor_tensor(rz[:, :], CT[par][:, :], rz[:, :], ALU.mult).then_inc(ctx_ready, 1)

                def accumulate(g, u):
                    dve.wait_ge(wo_ready, g + 1)
                    cs = slice(u * CH, (u + 1) * CH)
                    need(dve, sum_ready, g - NC + 1)
                    nc.vector.tensor_tensor(sT[:, cs], MV[:, :], sT[:, cs], ALU.add).then_inc(sum_ready, 1)

                nc.vector.tensor_copy(identr[:, :], ident[:, :])
                nc.vector.tensor_copy(ident16[:, :], ident[:, :])
                split_weights(0, 0)
                m = 0
                for n, (kind, c) in enumerate(start_jobs):
                    low(kind, 0, c, n, m)
                    m += kind != "v"
                    if n in (1, 5):
                        table_far(0, 0, n // 4)
                        for side in range(2):
                            table_side(0, n // 4, side)
                for m in range(2 * TC * NC):
                    reduce(0, m)
                dve.wait_ge(const_ready, 6)
                combine(0, 0, 0)
                rows(0, 0)
                start_links = links[0]
                body_links = 2 * 2 * 4 + BODY * 2

                def body(it, first, last):
                    links[:] = [0, start_links + it * body_links]
                    for l in range(BODY):
                        b, u = l // NC, l % NC
                        g, p = it * BODY + l, it * 2 + b
                        nb, nu = (l + 1) % BODY // NC, (l + 1) % NC
                        final, opening = last and l == BODY - 1, first and l == 0
                        todo = {slot: (kind, c, n, m) for kind, slot, c, n, m in jobs(it, l, last)}
                        for s in range(NT):
                            if not final:
                                for m in chunks_of(s):
                                    reduce((g + 1) * 2 * TC * NC, m)
                            if not opening:
                                if 3 <= s <= 6:
                                    ins = invert(g - 1, s - 3)
                                if s == 6:
                                    link(ins)
                                    normalise(g - 1, (l - 1) % 2)
                                if s == 9:
                                    accumulate(g - 1, (u - 1) % NC)
                            elif s == 6:
                                links[0] += 1
                                dve.sem_inc(chain, 1)
                            if s in todo:
                                kind, c, n, m = todo[s]
                                low(kind, 1 - b, (u + 2) % NC if kind == "q" else c, n, m)
                            if not (last and b):
                                if u == 0 and s == 10:
                                    split_weights(p + 1, 1 - b)
                                if u in (1, 2) and s == 7:
                                    table_far(p + 1, 1 - b, u - 1)
                                if u in (1, 2) and s in (8, 10):
                                    table_side(1 - b, u - 1, (s - 8) // 2)
                            if s == 12 and not final:
                                combine(g + 1, nb, nu)
                            if s == 14 and not final:
                                rows(g + 1, nu)
                    assert last or links[0] == body_links, (links, body_links)
                loop(dve, body)
                for i in range(TC):
                    ins = invert(NUNIT - 1, i)
                link(ins)
                normalise(NUNIT - 1, 1)
                accumulate(NUNIT - 1, NC - 1)


def finish(nc, x, silu_d, ident, sT, out):
    with ExitStack() as ctx:
        t_ = lambda name, shape, dt=F32: ctx.enter_context(nc.sbuf_tensor(name, shape, dt))
        s_ = lambda name: ctx.enter_context(nc.semaphore(name))
        ps = [ctx.enter_context(nc.psum_tensor(f"op{i}", [P, CH], F32)) for i in range(NC)]
        xt, gt, pt = t_("xt2", [P, NT, D]), t_("gt", [P, S]), t_("pt", [P, S])
        x_in, g_in = [s_(f"o_x{c}") for c in range(NC)], [s_(f"o_g{c}") for c in range(NC)]
        prod_ready, t_ready, o_ready, stored = s_("o_prod"), s_("o_t"), s_("o_sum"), s_("o_stored")
        xv = x.rearrange("o (t p) d -> p (o t) d", p=P)
        ov = out.rearrange("o (t p) d -> p (o t) d", p=P)
        with nc.Block() as block:
            @block.sync
            def _(sp):
                for c in range(NC):
                    sp.dma_start(gt[:, c * CH:(c + 1) * CH], silu_d[:, c * CH:(c + 1) * CH]).then_inc(g_in[c], 16)
                    sp.dma_start(xt[:, c * TC:(c + 1) * TC, :], xv[:, c * TC:(c + 1) * TC, :]).then_inc(x_in[c], 16)
                for c in range(NC):
                    sp.wait_ge(o_ready, c + 1)
                    sp.dma_start(ov[:, c * TC:(c + 1) * TC, :], xt[:, c * TC:(c + 1) * TC, :]).then_inc(stored, 16)
                sp.wait_ge(stored, 16 * NC)

            @block.vector
            def _(dve):
                for c in range(NC):
                    cs = slice(c * CH, (c + 1) * CH)
                    dve.wait_ge(g_in[c], 16)
                    nc.vector.tensor_tensor(pt[:, cs], sT[:, cs], gt[:, cs], ALU.mult).then_inc(prod_ready, 1)
                for c in range(NC):
                    dve.wait_ge(x_in[c], 16)
                    dve.wait_ge(t_ready, c + 1)
                    ts = slice(c * TC, (c + 1) * TC)
                    nc.vector.tensor_tensor(xt[:, ts, :], ps[c][:, :].rearrange("p (t d) -> p t d", t=TC), xt[:, ts, :],
                                            ALU.add).then_inc(o_ready, 1)

            @block.tensor
            def _(pe):
                for c in range(NC):
                    pe.wait_ge(prod_ready, c + 1)
                    for i in range(TC):
                        at = slice((c * TC + i) * P, (c * TC + i + 1) * P)
                        last = nc.tensor.transpose(ps[c][:, i * P:(i + 1) * P], pt[:, at], ident[:, :])
                    last.then_inc(t_ready, 1)


def build(nc, x, wq, wk, wv, wo, emb, wr, br, w1, b1, w2, b2, onehot, ident_c, mask_c, out):
    vec = nc.dram_tensor("bias_by_distance", [2, H, CH], F32, kind="Internal").ap()
    tabs = [nc.dram_tensor(f"bias_window{a}", [H, P, NEAR], F32, kind="Internal").ap() for a in range(2)]
    gates_d = nc.dram_tensor("gates", [E, S], F32, kind="Internal").ap()
    silu_d = nc.dram_tensor("silu", [D, S], F32, kind="Internal").ap()
    with ExitStack() as ctx:
        ident = ctx.enter_context(nc.sbuf_tensor("ident", [P, P], F32))
        sT = ctx.enter_context(nc.sbuf_tensor("sT", [P, S], F32))
        with nc.sbuf_tensor("xh", [P, S], F32R) as xh, nc.sbuf_tensor("xl", [P, S], F32R) as xl:
            prepare(nc, x, emb, onehot, ident_c, wr, br, xh, xl, ident, vec, tabs, gates_d)
            experts(nc, w1, b1, w2, b2, xh, xl, gates_d, silu_d)
            attention(nc, wq, wk, wv, wo, tabs, mask_c, xh, xl, ident, sT)
        finish(nc, x, silu_d, ident, sT, out)


_INS = ["L0_attn_hidden_states", "L0_attn_Wq", "L0_attn_Wk", "L0_attn_Wv", "L0_attn_Wo", "L0_attn_rel_bias_emb",
        "L0_ffn_Wr", "L0_ffn_br", "L0_ffn_W1", "L0_ffn_b1", "L0_ffn_W2", "L0_ffn_b2"]


def constants():
    import numpy as np
    starts = [0, 1, 2, 3, 4, 5, 6, 7, 8, 12, 16, 23, 32, 46, 64, 91]
    onehot = np.zeros((32, 2, 512), np.float32)
    for j in range(511):
        for a, rel in enumerate((255 - j, j - 255)):
            size = max(b for b in range(16) if starts[b] <= abs(rel))
            onehot[size + 16 * (rel > 0), a, j] = 1.0
    ident = np.eye(128, dtype=np.float32)
    mask = np.zeros((128, 16, 4), np.float32)
    for t in range(16):
        for c in range(4):
            mask[:, t, c] = float(t - 4 * c <= 1)
    return {"onehot": onehot, "ident": ident, "mask": mask}


def kernel(**inputs):
    import numpy as _np
    import concourse.bacc as _bacc
    from concourse import mybir as _mybir
    from concourse.bass_utils import run_bass_kernel_spmd as _run

    nc = _bacc.Bacc("TRN2", target_bir_lowering=False, num_devices=1)
    arrays, args = {}, []
    given = {n: inputs[n] for n in _INS}
    given.update(constants())
    for name, a in given.items():
        a = _np.ascontiguousarray(a)
        arrays[f"in_{name}"] = a
        args.append(nc.dram_tensor(f"in_{name}", a.shape, _mybir.dt.from_np(a.dtype), kind="ExternalInput").ap())
    args.append(nc.dram_tensor("out_0", (1, 2048, 128), _mybir.dt.float32, kind="ExternalOutput").ap())
    build(nc, *args)
    r = _run(nc, [arrays], core_ids=[0])
    return r.results[0]["out_0"]
```

```python
import concourse.bass as bass
from concourse import mybir
from contextlib import ExitStack

P = 128
S, D = 2048, 128
H, DK = 16, 64
NT = S // P
CH = 512
NC = S // CH
TC = CH // P
E, FF = 8, 512
NJ = FF // P
NPAIR = H // 2
NEAR = 3 * P
SAT = 91
BODY = 2 * NC
NUNIT = NPAIR * NC
NITER = NUNIT // BODY
RING = 8
EPS = 1e-5

F32, F32R, F16 = mybir.dt.float32, mybir.dt.float32r, mybir.dt.float16
ALU = mybir.AluOpType
ACT = mybir.ActivationFunctionType
AX = mybir.AxisListType.X


def need(eng, sem, value):
    if not isinstance(value, int) or value > 0:
        eng.wait_ge(sem, value)


def raw(ap):
    return ap.bitcast(F32)


def prepare(nc, x, emb, onehot, ident_c, wr, br, xh, xl, ident, vec, tabs, gates_d):
    with ExitStack() as ctx:
        t_ = lambda name, shape, dt=F32: ctx.enter_context(nc.sbuf_tensor(name, shape, dt))
        s_ = lambda name: ctx.enter_context(nc.semaphore(name))
        ps = [ctx.enter_context(nc.psum_tensor(f"pp{i}", [P, CH], F32)) for i in range(8)]
        xt, xn = t_("xt", [P, NT, D]), t_("xn", [P, NT, D])
        st, mv = t_("st", [P, NT, 6]), t_("mv", [P, NT, 2])
        va, sd, rs, t1, t2 = (t_(n, [P, NT]) for n in ("va", "sd", "rs", "t1", "t2"))
        emb_s, oh = t_("emb_s", [32, H]), t_("oh", [32, 2, CH])
        u_s = t_("u_s", [H, 2, CH])
        wr_s, wrh, wrl = t_("wr_s", [P, E]), t_("wrh", [P, P], F32R), t_("wrl", [P, P], F32R)
        lgT = t_("lgT", [E, S])
        br_s = t_("br_s", [P, E])
        lg, sel, cmp_, ex = (t_(n, [P, NT, E]) for n in ("lg", "sel", "cmp", "ex"))
        m1, z1 = t_("m1", [P, NT]), t_("z1", [P, NT])
        g8 = t_("g8", [E, S])
        s_x, s_c, s_o = s_("a_x"), s_("a_const"), s_("a_store")
        var_ready, sd_ready, xn_ready = s_("a_var"), s_("a_sd"), s_("a_xn")
        xt_ready, xh_ready, xl_ready = s_("a_xt"), s_("a_xh"), s_("a_xl")
        u_ready, u_saved, wr_ready = s_("a_u"), s_("a_usaved"), s_("a_wr")
        lgT_ready, lgT_saved = s_("a_lgT"), s_("a_lgTsaved")
        lg_ready, mm_ready, ex_ready, gate_ready = s_("a_lg"), s_("a_shift"), s_("a_ex"), s_("a_gate")
        g8_ready, g8_saved, chain = s_("a_g8"), s_("a_g8saved"), s_("a_chain")
        vec_done = s_("a_vec")
        with nc.Block() as block:
            @block.sync
            def _(sp):
                sp.dma_start(xt[:, :, :], x.rearrange("o (t p) d -> p (o t) d", p=P)).then_inc(s_x, 16)
                sp.dma_start(emb_s[:, :], emb).then_inc(s_c, 16)
                sp.dma_start(oh[:, :, :], onehot).then_inc(s_c, 16)
                sp.dma_start(ident[:, :], ident_c).then_inc(s_c, 16)
                sp.dma_start(wr_s[:, :], wr).then_inc(s_c, 16)
                sp.dma_start(br_s[:, :], br.partition_broadcast(P)).then_inc(s_c, 16)
                sp.wait_ge(u_saved, 2)
                sp.dma_start(vec.rearrange("a h n -> h a n"), u_s[:, :, :]).then_inc(vec_done, 16)
                sp.wait_ge(vec_done, 16)
                for a in range(2):
                    window = bass.AP(tensor=vec.tensor, offset=a * H * CH + P - 1,
                                     ap=[[CH, H], [-1, P], [1, NEAR]])
                    sp.dma_start(tabs[a], window).then_inc(s_o, 16)
                sp.wait_ge(g8_saved, NC)
                sp.dma_start(gates_d, g8[:, :]).then_inc(s_o, 16)
                sp.wait_ge(s_o, 48)

            @block.vector
            def _(dve):
                done = [0]

                def link(ins):
                    done[0] += 1
                    ins.then_inc(chain, 1)
                    dve.wait_ge(chain, done[0])

                nc.vector.memset(raw(wrh[:, :]), 0.0)
                link(nc.vector.memset(raw(wrl[:, :]), 0.0))
                dve.wait_ge(s_c, 80)
                link(nc.vector.tensor_copy(wrh[:, 0:E], wr_s[:, :]))
                nc.vector.tensor_tensor(wrl[:, 0:E], wr_s[:, :], raw(wrh[:, 0:E]), ALU.subtract).then_inc(wr_ready, 1)
                dve.wait_ge(s_x, 16)
                for t in range(NT):
                    last = nc.vector.bn_stats(st[:, t, :], xt[:, t, :])
                link(last)
                for t in range(NT):
                    last = nc.vector.bn_aggr(mv[:, t, :], st[:, t, :])
                link(last)
                nc.vector.tensor_scalar(va[:, :], mv[:, :, 1], EPS, None, ALU.add).then_inc(var_ready, 1)
                dve.wait_ge(sd_ready, 1)
                link(nc.vector.reciprocal(rs[:, :], sd[:, :]))
                link(nc.vector.tensor_tensor(t1[:, :], rs[:, :], rs[:, :], ALU.mult))
                link(nc.vector.tensor_tensor(t2[:, :], t1[:, :], va[:, :], ALU.mult))
                link(nc.vector.tensor_scalar(t1[:, :], t2[:, :], -0.5, 1.5, ALU.mult, ALU.add))
                link(nc.vector.tensor_tensor(sd[:, :], rs[:, :], t1[:, :], ALU.mult))
                for t in range(NT):
                    nc.vector.tensor_scalar(xn[:, t, :], xt[:, t, :], mv[:, t, 0:1], sd[:, t:t + 1],
                                            ALU.subtract, ALU.mult).then_inc(xn_ready, 1)
                for c in range(NC):
                    dve.wait_ge(xh_ready, c + 1)
                    nc.vector.tensor_tensor(xl[:, c * CH:(c + 1) * CH], ps[c][:, :],
                                            raw(xh[:, c * CH:(c + 1) * CH]), ALU.subtract).then_inc(xl_ready, 1)
                dve.wait_ge(u_ready, 1)
                for a in range(2):
                    nc.vector.tensor_copy(u_s[:, a, :], ps[4 + a][0:H, :]).then_inc(u_saved, 1)
                for c in range(NC):
                    dve.wait_ge(lgT_ready, c + 1)
                    nc.vector.tensor_copy(lgT[:, c * CH:(c + 1) * CH], ps[c][0:E, :]).then_inc(lgT_saved, 1)
                dve.wait_ge(lg_ready, 1)
                link(nc.vector.tensor_tensor(lg[:, :, :], ps[6][:, 0:NT * E].rearrange("p (t e) -> p t e", e=E),
                                             br_s[:, :].unsqueeze(1).to_broadcast([P, NT, E]), ALU.add))
                link(nc.vector.reduce_max(m1[:, :], lg[:, :, :], AX))
                link(nc.vector.tensor_tensor(ex[:, :, :], lg[:, :, :],
                                             m1[:, :].unsqueeze(2).to_broadcast([P, NT, E]), ALU.subtract))
                nc.vector.memset(sel[:, :, :], 0.0).then_inc(mm_ready, 1)
                for o in range(E):
                    for lo, hi, op in ((0, o, ALU.is_gt), (o, E, ALU.is_ge)):
                        if hi > lo:
                            other = lg[:, :, o:o + 1].to_broadcast([P, NT, hi - lo])
                            last = nc.vector.tensor_tensor(cmp_[:, :, lo:hi], other, lg[:, :, lo:hi], op)
                    link(last)
                    link(nc.vector.tensor_tensor(sel[:, :, :], sel[:, :, :], cmp_[:, :, :], ALU.add))
                link(nc.vector.tensor_scalar(sel[:, :, :], sel[:, :, :], 2.5, None, ALU.is_lt))
                dve.wait_ge(ex_ready, 1)
                link(nc.vector.tensor_tensor(ex[:, :, :], ex[:, :, :], sel[:, :, :], ALU.mult))
                link(nc.vector.reduce_sum(z1[:, :], ex[:, :, :], AX))
                link(nc.vector.reciprocal(m1[:, :], z1[:, :]))
                nc.vector.tensor_tensor(sel[:, :, :], ex[:, :, :],
                                        m1[:, :].unsqueeze(2).to_broadcast([P, NT, E]), ALU.mult).then_inc(gate_ready, 1)
                for c in range(NC):
                    dve.wait_ge(g8_ready, c + 1)
                    nc.vector.tensor_copy(g8[:, c * CH:(c + 1) * CH], ps[c][0:E, :]).then_inc(g8_saved, 1)

            @block.scalar
            def _(act):
                act.wait_ge(var_ready, 1)
                nc.scalar.activation(sd[:, :], va[:, :], ACT.Sqrt).then_inc(sd_ready, 1)
                for c in range(NC):
                    act.wait_ge(xt_ready, c + 1)
                    nc.scalar.activation(xh[:, c * CH:(c + 1) * CH], ps[c][:, :], ACT.Copy).then_inc(xh_ready, 1)
                act.wait_ge(mm_ready, 1)
                nc.scalar.activation(ex[:, :, :], ex[:, :, :], ACT.Exp).then_inc(ex_ready, 1)

            @block.tensor
            def _(pe):
                pe.wait_ge(s_c, 80)
                for a in range(2):
                    last = nc.tensor.matmul(ps[4 + a][0:H, :], emb_s[:, :], oh[:, a, :], start=True, stop=True)
                last.then_inc(u_ready, 1)
                for c in range(NC):
                    pe.wait_ge(xn_ready, (c + 1) * TC)
                    for i in range(TC):
                        last = nc.tensor.transpose(ps[c][:, i * P:(i + 1) * P], xn[:, c * TC + i, :], ident[:, :])
                    last.then_inc(xt_ready, 1)
                pe.wait_ge(wr_ready, 1)
                for c in range(NC):
                    pe.wait_ge(xl_ready, c + 1)
                    parts = [(a, b) for a in (wrh, wrl) for b in (xh, xl)]
                    for n, (a, b) in enumerate(parts):
                        last = nc.tensor.matmul(ps[c][:, :], a[:, :], b[:, c * CH:(c + 1) * CH], start=n == 0, stop=n == 3)
                    last.then_inc(lgT_ready, 1)
                for t in range(NT):
                    pe.wait_ge(lgT_saved, t // TC + 1)
                    last = nc.tensor.transpose(ps[6][:, t * E:(t + 1) * E], lgT[:, t * P:(t + 1) * P], ident[0:E, 0:E])
                last.then_inc(lg_ready, 1)
                pe.wait_ge(gate_ready, 1)
                for c in range(NC):
                    for i in range(TC):
                        last = nc.tensor.transpose(ps[c][0:E, i * P:(i + 1) * P], sel[:, c * TC + i, :], ident[:, :])
                    last.then_inc(g8_ready, 1)


def experts(nc, w1, b1, w2, b2, xh, xl, gates_d, moe_d):
    with ExitStack() as ctx:
        t_ = lambda name, shape, dt=F32: ctx.enter_context(nc.sbuf_tensor(name, shape, dt))
        s_ = lambda name: ctx.enter_context(nc.semaphore(name))
        hp = [ctx.enter_context(nc.psum_tensor(f"hp{i}", [P, CH], F32)) for i in range(NJ)]
        yp = [ctx.enter_context(nc.psum_tensor(f"yp{i}", [P, CH], F32)) for i in range(2)]
        w1r, w2r = t_("w1r", [P, 2, FF]), t_("w2r", [P, 2, NJ, D])
        w1h, w1l = t_("w1h", [P, 2, FF], F32R), t_("w1l", [P, 2, FF], F32R)
        w2h, w2l = t_("w2h", [P, 2, NJ * D], F32R), t_("w2l", [P, 2, NJ * D], F32R)
        b1s, b2s = t_("b1s", [P, 2, NJ]), t_("b2s", [P, 2, 1])
        gb = t_("gb", [P, 2, S])
        h32 = t_("h32", [P, 2, NJ, CH])
        hh, hl = t_("hh", [P, 2, NJ, CH], F32R), t_("hl", [P, 2, NJ, CH], F32R)
        yg = t_("yg", [P, 2, CH])
        fT = t_("fT", [P, S])
        loaded = [s_("f_loaded0"), s_("f_loaded1")]
        hi_split, split, stored = s_("f_hi_split"), s_("f_split"), s_("f_stored")
        gload = [s_("f_gload0"), s_("f_gload1")]
        hp_ready, h32_ready, h_ready, yp_ready = s_("f_hp"), s_("f_h32"), s_("f_h"), s_("f_yp")
        hh_ready, yg_ready, sum_done = s_("f_hh"), s_("f_yg"), s_("f_sum")
        bodies = 2 * NC

        def loop(eng, body):
            body(0, True, False)
            with eng.Fori(1, E // 2 - 1) as it:
                body(it, False, False)
            body(E // 2 - 1, False, True)

        with nc.Block() as block:
            @block.sync
            def _(sp):
                def body(it, first, last):
                    for b in range(2):
                        e = it * 2 + b
                        need(sp, yg_ready, (e - 1) * NC)
                        sp.dma_start(w1r[:, b, :], w1[bass.ds(e, 1), :, :].rearrange("e d h -> d (e h)")).then_inc(loaded[b], 16)
                        sp.dma_start(w2r[:, b, :, :], w2[bass.ds(e, 1), :, :].rearrange("e (j p) o -> p (e j) o", p=P)).then_inc(loaded[b], 16)
                        sp.dma_start(b1s[:, b, :], b1[bass.ds(e, 1), :].rearrange("e (j p) -> p (e j)", p=P), allow_slow_non_contiguous=True).then_inc(loaded[b], 16)
                        sp.dma_start(b2s[:, b, :], b2[bass.ds(e, 1), :].rearrange("e p -> p e"), allow_slow_non_contiguous=True).then_inc(loaded[b], 16)
                        g = bass.AP(tensor=gates_d.tensor, offset=e * S, ap=[[0, P], [1, S]])
                        sp.dma_start(gb[:, b, :], g).then_inc(gload[b], 16)
                loop(sp, body)
                for c in range(NC):
                    cs = slice(c * CH, (c + 1) * CH)
                    sp.wait_ge(sum_done, E * NC - NC + c + 2)
                    sp.dma_start(moe_d[:, cs], fT[:, cs]).then_inc(stored, 16)
                sp.wait_ge(stored, 16 * NC)

            @block.gpsimd
            def _(pool):
                nc.gpsimd.memset(fT[:, :], 0.0).then_inc(sum_done, 1)

                def add(n, c):
                    pool.wait_ge(yg_ready, n + 1)
                    pool.wait_ge(sum_done, n + 1)
                    nc.gpsimd.tensor_tensor(fT[:, c * CH:(c + 1) * CH], fT[:, c * CH:(c + 1) * CH],
                                            yg[:, c % 2, :], ALU.add).then_inc(sum_done, 1)

                def body(it, first, last):
                    for b in range(2):
                        e = it * 2 + b
                        need(pool, yp_ready, (e - 1) * NC)
                        w2f = w2r[:, b, :, :].rearrange("p j o -> p (j o)")
                        pool.wait_ge(hi_split, e * 2 + 2)
                        nc.gpsimd.tensor_tensor(w1l[:, b, :], w1r[:, b, :], raw(w1h[:, b, :]), ALU.subtract).then_inc(split, 1)
                        nc.gpsimd.tensor_tensor(w2l[:, b, :], w2f, raw(w2h[:, b, :]), ALU.subtract).then_inc(split, 1)
                        for c in range(NC):
                            if not (first and b == 0):
                                add((e - 1) * NC + c, c)
                loop(pool, body)
                for c in range(NC):
                    add((E - 1) * NC + c, c)

            @block.tensor
            def _(pe):
                def up(it, b, c):
                    e = it * 2 + b
                    n = e * NC + c
                    if c == 0:
                        pe.wait_ge(split, e * 2 + 1)
                    for j in range(NJ):
                        need(pe, h32_ready, (n - 1) * NJ + j + 1)
                        w = slice(j * P, (j + 1) * P)
                        xs = slice(c * CH, (c + 1) * CH)
                        nc.tensor.matmul(hp[j][:, :], w1h[:, b, w], xh[:, xs], start=True, stop=False)
                        nc.tensor.matmul(hp[j][:, :], w1l[:, b, w], xh[:, xs], start=False, stop=False)
                        nc.tensor.matmul(hp[j][:, :], w1h[:, b, w], xl[:, xs], start=False, stop=True).then_inc(hp_ready, 1)

                def down(it, b, c):
                    n = (it * 2 + b) * NC + c
                    if c == 0:
                        pe.wait_ge(split, (it * 2 + b) * 2 + 2)
                    need(pe, yg_ready, n - 1)
                    for j in range(NJ):
                        pe.wait_ge(h_ready, n * NJ + j + 1)
                        w = slice(j * P, (j + 1) * P)
                        nc.tensor.matmul(yp[c % 2][:, :], w2h[:, b, w], hh[:, c % 2, j, :], start=j == 0, stop=False)
                        nc.tensor.matmul(yp[c % 2][:, :], w2l[:, b, w], hh[:, c % 2, j, :], start=False, stop=False)
                        last = nc.tensor.matmul(yp[c % 2][:, :], w2h[:, b, w], hl[:, c % 2, j, :], start=False, stop=j == NJ - 1)
                    last.then_inc(yp_ready, 1)

                def body(it, first, last):
                    for b in range(2):
                        for c in range(NC):
                            up(it, b, c)
                            if c:
                                down(it, b, c - 1)
                            elif b:
                                down(it, 0, NC - 1)
                            elif not first:
                                down(it - 1, 1, NC - 1)
                loop(pe, body)
                down(E // 2 - 1, 1, NC - 1)

            @block.scalar
            def _(act):
                def split_high(it, b):
                    act.wait_ge(loaded[b], (it + 1) * 64)
                    need(act, yp_ready, (it * 2 + b - 1) * NC)
                    nc.scalar.activation(w1h[:, b, :], w1r[:, b, :], ACT.Copy).then_inc(hi_split, 1)
                    nc.scalar.activation(w2h[:, b, :], w2r[:, b, :, :].rearrange("p j o -> p (j o)"),
                                         ACT.Copy).then_inc(hi_split, 1)

                split_high(0, 0)

                def body(it, first, last):
                    for b in range(2):
                        e = it * 2 + b
                        for c in range(NC):
                            if c == 2 and not (last and b):
                                split_high(it + b, 1 - b)
                            n = e * NC + c
                            for j in range(NJ):
                                act.wait_ge(hp_ready, n * NJ + j + 1)
                                need(act, h_ready, (n - 2) * NJ + j + 1)
                                nc.scalar.activation(h32[:, c % 2, j, :], hp[j][:, :], ACT.Relu,
                                                     bias=b1s[:, b, j:j + 1]).then_inc(h32_ready, 1)
                loop(act, body)

            @block.vector
            def _(dve):
                def halves(it, b, c):
                    n = (it * 2 + b) * NC + c
                    for j in range(NJ):
                        dve.wait_ge(h32_ready, n * NJ + j + 1)
                        if j == 0:
                            need(dve, yp_ready, n - 1)
                        nc.vector.tensor_copy(hh[:, c % 2, j, :], h32[:, c % 2, j, :]).then_inc(hh_ready, 1)
                        dve.wait_ge(hh_ready, n * NJ + j + 1)
                        nc.vector.tensor_tensor(hl[:, c % 2, j, :], h32[:, c % 2, j, :],
                                                raw(hh[:, c % 2, j, :]), ALU.subtract).then_inc(h_ready, 1)

                def gated(it, b, c):
                    e = it * 2 + b
                    n = e * NC + c
                    if c == 0:
                        dve.wait_ge(gload[b], (it + 1) * 16)
                        dve.wait_ge(loaded[b], (it + 1) * 64)
                    dve.wait_ge(yp_ready, n + 1)
                    need(dve, sum_done, n)
                    nc.vector.scalar_tensor_tensor(out=yg[:, c % 2, :], in0=yp[c % 2][:, :], scalar=b2s[:, b, 0:1],
                                                   in1=gb[:, b, c * CH:(c + 1) * CH], op0=ALU.add,
                                                   op1=ALU.mult).then_inc(yg_ready, 1)

                def body(it, first, last):
                    for b in range(2):
                        for c in range(NC):
                            halves(it, b, c)
                            if c:
                                gated(it, b, c - 1)
                            elif b:
                                gated(it, 0, NC - 1)
                            elif not first:
                                gated(it - 1, 1, NC - 1)
                loop(dve, body)
                gated(E // 2 - 1, 1, NC - 1)


def near_columns(r):
    start = (r - 1) * P
    lo = max(start if r <= 1 else start + P - SAT + 1, 0)
    hi = min(start + 2 * P + SAT - 1 if r <= 1 else start + NEAR, CH)
    return slice(lo, hi), slice(lo - start, hi - start)


def chunks_of(s):
    full = 2 * TC * NC
    return list(range(min(s * full // 14, full), min((s + 1) * full // 14, full)))


def attention(nc, wq, wk, wv, wo, tabs, mask_c, xh, xl, ident, moe_d, silu_d, sT):
    with ExitStack() as ctx:
        t_ = lambda name, shape, dt=F32: ctx.enter_context(nc.sbuf_tensor(name, shape, dt))
        s_ = lambda name: ctx.enter_context(nc.semaphore(name))
        bank = lambda name: ctx.enter_context(nc.psum_tensor(name, [P, CH], F32))
        SM = [bank("SM0"), bank("SM1")]
        ST = [bank("ST0"), bank("ST1")]
        CT = [bank("CT0"), bank("CT1")]
        MV = bank("MV")
        MP = bank("MP")
        Q1 = [t_(f"Q1{h}", [P, S], F32R) for h in range(2)]
        Q2 = [t_(f"Q2{h}", [P, S], F32R) for h in range(2)]
        K1 = [[t_(f"K1{b}{h}", [P, S], F32R) for h in range(2)] for b in range(2)]
        K2 = [[t_(f"K2{b}{h}", [P, S], F32R) for h in range(2)] for b in range(2)]
        V = [t_(f"V{b}", [P, NT, 2 * DK]) for b in range(2)]
        PR = t_("PR", [P, RING, CH])
        Z = t_("Z", [P, 2, 2, CH])
        rz = t_("rz", [P, CH])
        TR = t_("TR", [P, 2, NEAR])
        TH = t_("TH", [P, 2, 2, 2, NEAR], F32R)
        TL = t_("TL", [P, 2, 2, 2, NEAR], F16)
        TM = t_("TM", [P, 2, 2, 2, NEAR], F32R)
        far = t_("far", [P, 2, 2, 2])
        fd = t_("fd", [P, 2])
        fm = t_("fm", [P, 2, 2, NT, NC])
        WR, WH, WL = t_("WR", [P, 3 * P]), t_("WH", [P, 2, 3 * P], F32R), t_("WL", [P, 2, 3 * P], F32R)
        WO = t_("WO", [P, 2, D])
        identr, ident16 = t_("identr", [P, P], F32R), t_("ident16", [P, P], F16)
        ones = t_("ones", [P, DK])
        mask = t_("mask", [P, NT, NC])
        mx, mxb, nm = t_("mx", [P, 2, TC, NC]), t_("mxb", [P, 2, TC, NC]), t_("nm", [P, 2, TC])

        w_loaded, t_loaded, c_loaded = s_("w_loaded"), s_("t_loaded"), s_("c_loaded")
        wo_loaded = [s_("wo_loaded0"), s_("wo_loaded1")]
        q_copied = [s_("q_copied0"), s_("q_copied1")]
        k_copied = [s_("k_copied0"), s_("k_copied1")]
        const_ready, wh_ready, wl_ready, tab_ready = s_("const_ready"), s_("wh_ready"), s_("wl_ready"), s_("tab_ready")
        mp_ready, hi_ready, mp_free = s_("mp_ready"), s_("hi_ready"), s_("mp_free")
        sm_ready, mx_ready, nm_ready = s_("sm_ready"), s_("mx_ready"), s_("nm_ready")
        mt_ready, rows_ready = s_("mt_ready"), s_("rows_ready")
        st_ready, exp_ready, pv_done, z_done = s_("st_ready"), s_("exp_ready"), s_("pv_done"), s_("z_done")
        zb_ready, ctx_ready, wo_ready, sum_ready = s_("zb_ready"), s_("ctx_ready"), s_("wo_ready"), s_("sum_ready")
        chain = s_("dve_chain")
        moe_loaded, moe_exp, silu_ready, silu_stored = s_("moe_loaded"), s_("moe_exp"), s_("silu_ready"), s_("silu_stored")

        job_list = {0: [("q", 13, 0)],
                    1: [("q", 5, 0), ("k", 7, 0), ("v", 9, 0), ("k", 11, 1), ("v", 13, 1)],
                    2: [("q", 5, 0), ("k", 7, 2), ("v", 9, 2), ("k", 11, 3), ("v", 13, 3)],
                    3: [("q", 13, 0)]}
        start_jobs = [("k", c) for c in range(4)] + [("v", c) for c in range(4)] + [("q", 0), ("q", 1)]

        start_banks = [ST[0], ST[1], CT[0], CT[1], MP, MV, SM[0], SM[1]]
        start_maxima = [SM[0], SM[1], CT[0], CT[1]]

        def jobs_before(l):
            full = [k for m in range(l) for k, _, _ in job_list[m % NC]]
            return len(full), sum(k != "v" for k in full)

        JOBS, HIGHS = jobs_before(BODY)

        def jobs(it, l, last):
            n, m = jobs_before(l)
            n, m = n + 10 + it * JOBS, m + 6 + it * HIGHS
            out = []
            for kind, slot, c in job_list[l % NC]:
                if last and (l >= NC and kind != "q" or l + 2 >= BODY):
                    continue
                out.append((kind, slot, c, n, m))
                n, m = n + 1, m + (kind != "v")
            return out

        def loop(eng, body):
            body(0, True, False)
            with eng.Fori(1, NITER - 1) as it:
                body(it, False, False)
            body(NITER - 1, False, True)

        with nc.Block() as block:
            @block.sync
            def _(sp):
                sp.dma_start(mask[:, :, :], mask_c).then_inc(c_loaded, 16)

                def weights(p):
                    cols = bass.ds(p * P, P)
                    for n, w in enumerate((wq, wk, wv)):
                        sp.dma_start(WR[:, n * P:(n + 1) * P], w[:, cols]).then_inc(w_loaded, 16)

                def table(p, h):
                    for a in range(2):
                        sp.dma_start(TR[:, a, :], tabs[a][bass.ds(p * 2 + h, 1), :, :].rearrange("h p n -> p (h n)")
                                     ).then_inc(t_loaded, 16)

                def load_wo(p, b):
                    sp.dma_start(WO[:, b, :], wo[bass.ds(p * P, P), :]).then_inc(wo_loaded[b], 16)

                def copy_q(u, m):
                    sp.wait_ge(hi_ready, m + 1)
                    for h in range(2):
                        cs = slice(u * CH, (u + 1) * CH)
                        sp.dma_start(raw(Q1[h][DK:P, cs]), raw(Q1[h][0:DK, cs])).then_inc(q_copied[u % 2], 16)

                def copy_k(b, c, m):
                    sp.wait_ge(hi_ready, m + 1)
                    for h in range(2):
                        cs = slice(c * CH, (c + 1) * CH)
                        sp.dma_start(raw(K2[b][h][0:DK, cs]), raw(K1[b][h][0:DK, cs])).then_inc(k_copied[b], 16)

                weights(0)
                table(0, 0)
                load_wo(0, 0)
                sp.wait_ge(tab_ready, 1)
                table(0, 1)
                for c in range(NC):
                    copy_k(0, c, c)
                for u in range(2):
                    copy_q(u, NC + u)

                def body(it, first, last):
                    for l in range(BODY):
                        b, u = l // NC, l % NC
                        p = it * 2 + b
                        more = not (last and b)
                        if u == 0 and more:
                            sp.wait_ge(wl_ready, p + 1)
                            weights(p + 1)
                            sp.wait_ge(tab_ready, p * 2 + 2)
                            table(p + 1, 0)
                        if u == 1 and more:
                            sp.wait_ge(wo_ready, it * BODY + l - 1)
                            load_wo(p + 1, 1 - b)
                        if u == 2 and more:
                            sp.wait_ge(tab_ready, p * 2 + 3)
                            table(p + 1, 1)
                        if first and l < NC:
                            need(sp, wo_ready, l)
                            sp.dma_start(rz[:, :], moe_d[:, u * CH:(u + 1) * CH]).then_inc(moe_loaded, 16)
                        for kind, _, c, _, m in jobs(it, l, last):
                            if kind == "k":
                                copy_k(1 - b, c, m)
                            elif kind == "q":
                                copy_q((u + 2) % NC, m)
                        if first and l < NC:
                            sp.wait_ge(silu_ready, l + 1)
                            sp.dma_start(silu_d[:, u * CH:(u + 1) * CH], rz[:, :]).then_inc(silu_stored, 16)
                loop(sp, body)
                sp.wait_ge(silu_stored, 16 * NC)

            @block.gpsimd
            def _(pool):
                nc.gpsimd.memset(sT[:, :], 0.0).then_inc(const_ready, 1)
                pool.wait_ge(const_ready, 1)
                nc.gpsimd.memset(ones[:, :], 1.0).then_inc(const_ready, 1)
                for b in range(2):
                    for h in range(2):
                        pool.wait_ge(const_ready, 2 + 2 * b + h)
                        nc.gpsimd.memset(raw(K2[b][h][DK:DK + TC, :]), 1.0).then_inc(const_ready, 1)

                def body(it, first, last):
                    for l in range(BODY):
                        g = it * BODY + l
                        z = Z[:, l % 2, :, :]
                        tile = lambda k: PR[:, 2 * k % RING:2 * k % RING + 2, :]
                        for s in range(1, NT):
                            pool.wait_ge(exp_ready, g * 2 * NT + 2 * s + 2)
                            if s == 1:
                                need(pool, zb_ready, g - 1)
                                a = tile(0)
                            else:
                                pool.wait_ge(z_done, g * (NT - 1) + s - 1)
                                a = z
                            nc.gpsimd.tensor_tensor(z, a, tile(s), ALU.add).then_inc(z_done, 1)
                loop(pool, body)

            @block.tensor
            def _(pe):
                def split_product(out, a, b, first=True, last=True):
                    nc.tensor.matmul(out, a[0], b[0], start=first, stop=False)
                    nc.tensor.matmul(out, a[1], b[0], start=False, stop=False)
                    return nc.tensor.matmul(out, a[0], b[1], start=False, stop=last)

                def project(kind, b, c, n, out=MP, behind=1):
                    need(pe, mp_free, n - behind + 1)
                    if kind == "v":
                        w = slice(2 * P, 3 * P)
                        for i in range(TC):
                            xs = slice((c * TC + i) * P, (c * TC + i + 1) * P)
                            last = split_product(out[:, i * P:(i + 1) * P], (xh[:, xs], xl[:, xs]),
                                                 (WH[:, b, w], WL[:, b, w]))
                    else:
                        w = slice(0, P) if kind == "q" else slice(P, 2 * P)
                        xs = slice(c * CH, (c + 1) * CH)
                        last = split_product(out[:, :], (WH[:, b, w], WL[:, b, w]), (xh[:, xs], xl[:, xs]))
                    last.then_inc(mp_ready, 1)

                def maxima(n0, b, u, m, banks=SM):
                    h, t, c = m // (TC * NC), m // NC % TC, m % NC
                    need(pe, mx_ready, n0 + m - len(banks) + 1)
                    T = u * TC + t
                    out = banks[m % len(banks)]
                    r = T - c * TC
                    near = -1 <= r <= TC
                    last = nc.tensor.matmul(out[:, :], Q1[h][:, T * P:(T + 1) * P], K1[b][h][:, c * CH:(c + 1) * CH],
                                            start=True, stop=not near)
                    if near:
                        cols, of_table = near_columns(r)
                        last = nc.tensor.matmul(out[:, cols], identr[:, :], TM[:, b, h, int(r <= 1), of_table],
                                                start=False, stop=True)
                    last.then_inc(sm_ready, 1)

                def ready_for_maxima(p, u, g, n_job):
                    pe.wait_ge(mp_free, n_job + 1)
                    pe.wait_ge(q_copied[u % 2], (p * 2 + u // 2 + 1) * 32)
                    if u == 0:
                        pe.wait_ge(tab_ready, p * 2 + 2)

                def turn(g):
                    pe.wait_ge(nm_ready, g + 1)
                    need(pe, sum_ready, g - 1)
                    for h in range(2):
                        last = nc.tensor.transpose(MV[0:TC, h * P:(h + 1) * P], nm[:, h, :], ident[:, :])
                    last.then_inc(mt_ready, 1)

                def scores(g, b, u, s, h):
                    need(pe, exp_ready, g * 2 * NT + 2 * s + h - 1)
                    ks, qs = slice(s * P, (s + 1) * P), slice(u * CH, (u + 1) * CH)
                    r = s - u * TC
                    near = -1 <= r <= TC
                    nc.tensor.matmul(ST[h][:, :], K1[b][h][:, ks], Q1[h][:, qs], start=True, stop=False)
                    last = nc.tensor.matmul(ST[h][:, :], K2[b][h][0:DK + TC, ks], Q2[h][0:DK + TC, qs],
                                            start=False, stop=not near)
                    if near:
                        side, (cols, of_table) = int(r > 1), near_columns(r)
                        nc.tensor.matmul(ST[h][:, cols], identr[:, :], TH[:, b, h, side, of_table],
                                         start=False, stop=False)
                        last = nc.tensor.matmul(ST[h][:, cols], ident16[:, :], TL[:, b, h, side, of_table],
                                                start=False, stop=True)
                    last.then_inc(st_ready, 1)

                def values(g, b, par, s, after_silu=False):
                    pe.wait_ge(exp_ready, g * 2 * NT + 2 * s + 2)
                    if s == 0:
                        need(pe, ctx_ready, g - 1)
                        if after_silu:
                            pe.wait_ge(silu_ready, g)
                    for h in range(2):
                        rows = slice(h * DK, (h + 1) * DK)
                        last = nc.tensor.matmul(CT[par][rows, :], V[b][:, s, rows], PR[:, (2 * s + h) % RING, :],
                                                start=s == 0, stop=s == NT - 1)
                    last.then_inc(pv_done, 1)

                def sums(g, par):
                    pe.wait_ge(z_done, (g + 1) * (NT - 1))
                    pe.wait_ge(rows_ready, g + 1)
                    for h in range(2):
                        last = nc.tensor.matmul(MV[h * DK:(h + 1) * DK, :], ones[:, :], Z[:, par, h, :],
                                                start=True, stop=True)
                    last.then_inc(zb_ready, 1)

                def output(g, b, it):
                    pe.wait_ge(ctx_ready, g + 1)
                    pe.wait_ge(wo_loaded[b], (it + 1) * 16)
                    nc.tensor.matmul(MV[:, :], WO[:, b, :], rz[:, :], start=True, stop=True).then_inc(wo_ready, 1)

                pe.wait_ge(wl_ready, 1)
                for n, (kind, c) in enumerate(start_jobs):
                    project(kind, 0, c, n, start_banks[n % 8], 8)
                ready_for_maxima(0, 0, 0, 9)
                for m in range(2 * TC * NC):
                    maxima(0, 0, 0, m, start_maxima)
                turn(0)

                def body(it, first, last):
                    for l in range(BODY):
                        b, u = l // NC, l % NC
                        g, p = it * BODY + l, it * 2 + b
                        nb, nu = (l + 1) % BODY // NC, (l + 1) % NC
                        lb, lit = ((l - 1) % BODY) // NC, it if l else it - 1
                        final = last and l == BODY - 1
                        todo = {slot: (kind, c, n) for kind, slot, c, n, _ in jobs(it, l, last)}
                        pe.wait_ge(rows_ready, g + 1)
                        if u == 0:
                            pe.wait_ge(k_copied[b], (it + 1) * 32 * NC)
                        if not final:
                            q_job = [n for kind, _, _, n, _ in jobs(it, l - 1, last) if kind == "q"][0] if l else 9 + it * JOBS
                            ready_for_maxima(it * 2 + (l + 1) // NC, nu, g + 1, q_job)
                        for s in range(NT):
                            chunks = [] if final else chunks_of(s)
                            for h in range(2):
                                scores(g, b, u, s, h)
                                for m in chunks[h:h + 1]:
                                    maxima((g + 1) * 2 * TC * NC, nb, nu, m)
                            if s:
                                values(g, b, l % 2, s - 1, first and 1 <= l <= NC)
                            elif not (first and l == 0):
                                values(g - 1, lb, (l - 1) % 2, NT - 1)
                            for m in chunks[2:]:
                                maxima((g + 1) * 2 * TC * NC, nb, nu, m)
                            if s == 14 and not final:
                                turn(g + 1)
                            if not (first and l == 0):
                                if s == 2:
                                    sums(g - 1, (l - 1) % 2)
                                if s == 8:
                                    output(g - 1, lb, lit)
                            if s in todo:
                                kind, c, n = todo[s]
                                if kind == "q":
                                    project("q", (l + 2) % BODY // NC, (u + 2) % NC, n)
                                else:
                                    project(kind, 1 - b, c, n)
                loop(pe, body)
                values(NUNIT - 1, 1, 1, NT - 1)
                pe.wait_ge(sum_ready, NUNIT - 1)
                sums(NUNIT - 1, 1)
                output(NUNIT - 1, 1, NITER - 1)

            @block.scalar
            def _(act):
                def split_weights(p, b):
                    act.wait_ge(w_loaded, (p + 1) * 48)
                    nc.scalar.activation(WH[:, b, :], WR[:, :], ACT.Copy).then_inc(wh_ready, 1)

                def high(kind, b, c, n, src=MP):
                    act.wait_ge(mp_ready, n + 1)
                    for h in range(2):
                        dst = Q1[h] if kind == "q" else K1[b][h]
                        last = nc.scalar.activation(dst[0:DK, c * CH:(c + 1) * CH], src[h * DK:(h + 1) * DK, :], ACT.Copy)
                    last.then_inc(hi_ready, 1)

                split_weights(0, 0)
                for n, (kind, c) in enumerate(start_jobs):
                    if kind != "v":
                        high(kind, 0, c, n, start_banks[n % 8])

                def body(it, first, last):
                    for l in range(BODY):
                        b, u = l // NC, l % NC
                        g, p = it * BODY + l, it * 2 + b
                        todo = {slot: (kind, c, n) for kind, slot, c, n, _ in jobs(it, l, last)}
                        if u == 0:
                            act.wait_ge(tab_ready, p * 2 + 2)
                        for s in range(NT):
                            for h in range(2):
                                n = g * 2 * NT + 2 * s + h
                                act.wait_ge(st_ready, n + 1)
                                if s >= 4 or not (first and l == 0):
                                    act.wait_ge(pv_done, g * NT + s - 3)
                                    if s >= 4:
                                        k = g * (NT - 1) + max(s - 5, 0) + 1
                                    else:
                                        k = (g - 1) * (NT - 1) + NT + s - 4
                                    act.wait_ge(z_done, k)
                                side = int(s - u * TC > 1)
                                nc.scalar.activation(PR[:, (2 * s + h) % RING, :], ST[h][:, :], ACT.Exp,
                                                     bias=far[:, b, h, side:side + 1]).then_inc(exp_ready, 1)
                            if s in todo and todo[s][0] != "v":
                                kind, c, n = todo[s]
                                high(kind, 1 - b, (u + 2) % NC if kind == "q" else c, n)
                            if s == 9 and u == 0 and not (last and b):
                                split_weights(p + 1, 1 - b)
                            if s == 10 and first and l < NC:
                                act.wait_ge(moe_loaded, (l + 1) * 16)
                                need(act, ctx_ready, l)
                                nc.scalar.activation(CT[1 - l % 2][:, :], rz[:, :], ACT.Exp, scale=-1.0).then_inc(moe_exp, 1)
                loop(act, body)

            @block.vector
            def _(dve):
                links = [0, None]

                def link(ins):
                    links[0] += 1
                    ins.then_inc(chain, 1)
                    dve.wait_ge(chain, links[0] if links[1] is None else links[1] + links[0])

                def split_weights(p, b):
                    dve.wait_ge(wh_ready, p + 1)
                    nc.vector.tensor_tensor(WL[:, b, :], WR[:, :], raw(WH[:, b, :]), ALU.subtract).then_inc(wl_ready, 1)

                def table_far(p, b, h):
                    dve.wait_ge(t_loaded, (p * 2 + h + 1) * 32)
                    nc.vector.tensor_copy(far[:, b, h, 0:1], TR[:, 0, NEAR - 1:NEAR])
                    link(nc.vector.tensor_copy(far[:, b, h, 1:2], TR[:, 0, 0:1]))
                    link(nc.vector.tensor_tensor(fd[:, h:h + 1], far[:, b, h, 1:2], far[:, b, h, 0:1], ALU.subtract))
                    dve.wait_ge(c_loaded, 16)
                    nc.vector.tensor_scalar(fm[:, b, h, :, :], mask[:, :, :], fd[:, h:h + 1], far[:, b, h, 0:1],
                                            ALU.mult, ALU.add)

                def table_side(b, h, side):
                    f = far[:, b, h, side:side + 1]
                    nc.vector.tensor_scalar(TM[:, b, h, side, :], TR[:, 1, :], f, None, ALU.subtract)
                    link(nc.vector.tensor_scalar(TH[:, b, h, side, :], TR[:, 0, :], f, None, ALU.subtract))
                    last = nc.vector.scalar_tensor_tensor(out=TL[:, b, h, side, :], in0=TR[:, 0, :], scalar=f,
                                                          in1=raw(TH[:, b, h, side, :]), op0=ALU.subtract,
                                                          op1=ALU.subtract)
                    if side:
                        last.then_inc(tab_ready, 1)

                def low(kind, b, c, n, m, part, src=MP):
                    if part == 0:
                        dve.wait_ge(mp_ready, n + 1)
                    if kind == "v":
                        if part == 0:
                            nc.vector.tensor_copy(V[b][:, c * TC:(c + 1) * TC, :],
                                                  src[:, :].rearrange("p (t d) -> p t d", t=TC)).then_inc(mp_free, 1)
                        return
                    if part == 0:
                        dve.wait_ge(hi_ready, m + 1)
                    cs = slice(c * CH, (c + 1) * CH)
                    dst, hi = ((Q2[part][0:DK, cs], Q1[part]) if kind == "q" else
                               (K1[b][part][DK:P, cs], K1[b][part]))
                    ins = nc.vector.tensor_tensor(dst, src[part * DK:(part + 1) * DK, :], raw(hi[0:DK, cs]), ALU.subtract)
                    if part:
                        ins.then_inc(mp_free, 1)

                def reduce(n0, m, banks=SM):
                    h, t, c = m // (TC * NC), m // NC % TC, m % NC
                    dve.wait_ge(sm_ready, n0 + m + 1)
                    nc.vector.reduce_max(mx[:, h, t, c:c + 1], banks[m % len(banks)][:, :], AX).then_inc(mx_ready, 1)

                def combine(g, b, u):
                    dve.wait_ge(mx_ready, (g + 1) * 2 * TC * NC)
                    link(nc.vector.tensor_tensor(mxb[:, :, :, :], mx[:, :, :, :], fm[:, b, :, u * TC:(u + 1) * TC, :], ALU.add))
                    nc.vector.tensor_reduce(nm[:, :, :], mxb[:, :, :, :], AX, ALU.max, negate=True).then_inc(nm_ready, 1)

                def rows(g, u):
                    dve.wait_ge(mt_ready, g + 1)
                    for h in range(2):
                        src = MV[0:TC, h * P:(h + 1) * P].unsqueeze(1).to_broadcast([TC, TC, P])
                        dst = Q2[h][DK:DK + TC, u * CH:(u + 1) * CH].rearrange("p (t q) -> p t q", t=TC)
                        own = ident[0:TC, 0:TC].unsqueeze(2).to_broadcast([TC, TC, P])
                        last = nc.vector.tensor_tensor(dst, src, own, ALU.mult)
                    last.then_inc(rows_ready, 1)

                def invert(g, i, after_silu=False):
                    if i == 0:
                        dve.wait_ge(zb_ready, g + 1)
                        need(dve, wo_ready, g)
                        if after_silu:
                            dve.wait_ge(silu_stored, (g + 1) * 16)
                    cs = slice(i * DK, (i + 1) * DK)
                    return nc.vector.reciprocal(rz[:, cs], MV[:, cs])

                def silu(l, i):
                    e = CT[1 - l % 2]
                    if i == 0:
                        dve.wait_ge(moe_exp, l + 1)
                        link(nc.vector.tensor_scalar(e[:, :], e[:, :], 1.0, None, ALU.add))
                    elif i < 5:
                        cs = slice((i - 1) * P, i * P)
                        ins = nc.vector.reciprocal(e[:, cs], e[:, cs])
                        if i == 4:
                            link(ins)
                    else:
                        nc.vector.tensor_tensor(rz[:, :], e[:, :], rz[:, :], ALU.mult).then_inc(silu_ready, 1)

                def normalise(g, par):
                    dve.wait_ge(pv_done, (g + 1) * NT)
                    nc.vector.tensor_tensor(rz[:, :], CT[par][:, :], rz[:, :], ALU.mult).then_inc(ctx_ready, 1)

                def accumulate(g, u):
                    dve.wait_ge(wo_ready, g + 1)
                    cs = slice(u * CH, (u + 1) * CH)
                    need(dve, sum_ready, g - NC + 1)
                    nc.vector.tensor_tensor(sT[:, cs], MV[:, :], sT[:, cs], ALU.add).then_inc(sum_ready, 1)

                nc.vector.tensor_copy(identr[:, :], ident[:, :])
                nc.vector.tensor_copy(ident16[:, :], ident[:, :])
                split_weights(0, 0)
                m = 0
                for n, (kind, c) in enumerate(start_jobs):
                    for part in range(2):
                        low(kind, 0, c, n, m, part, start_banks[n % 8])
                    m += kind != "v"
                    if n in (1, 5):
                        table_far(0, 0, n // 4)
                        for side in range(2):
                            table_side(0, n // 4, side)
                for m in range(2 * TC * NC):
                    reduce(0, m, start_maxima)
                dve.wait_ge(const_ready, 6)
                combine(0, 0, 0)
                rows(0, 0)
                start_links = links[0] + 2 * NC
                body_links = 2 * 2 * 4 + BODY * 2
                invert_at = [(3, 0), (3, 1), (3, 2), (4, 1), (4, 2), (5, 0), (5, 1), (5, 2)]
                silu_at = [(11, 1), (12, 0), (12, 2), (13, 0), (13, 1), (15, 0)]

                def body(it, first, last):
                    links[:] = [0, start_links - (2 * NC if first else 0) + it * body_links]
                    for l in range(BODY):
                        b, u = l // NC, l % NC
                        g, p = it * BODY + l, it * 2 + b
                        nb, nu = (l + 1) % BODY // NC, (l + 1) % NC
                        final, opening = last and l == BODY - 1, first and l == 0
                        todo = {slot: (kind, c, n, m) for kind, slot, c, n, m in jobs(it, l, last)}
                        with_silu = first and l < NC
                        for s in range(NT):
                            chunks = [] if final else chunks_of(s)
                            for k in range(3):
                                for m in chunks[k:k + 1]:
                                    reduce((g + 1) * 2 * TC * NC, m)
                                if not opening:
                                    if (s, k) in invert_at:
                                        ins = invert(g - 1, invert_at.index((s, k)), first and l <= NC)
                                    if (s, k) == (6, 0):
                                        link(ins)
                                        normalise(g - 1, (l - 1) % 2)
                                    if (s, k) == (9, 1):
                                        accumulate(g - 1, (u - 1) % NC)
                                elif (s, k) == (6, 0):
                                    links[0] += 1
                                    dve.sem_inc(chain, 1)
                                if s - 1 in todo and k:
                                    kind, c, n, m = todo[s - 1]
                                    low(kind, 1 - b, (u + 2) % NC if kind == "q" else c, n, m, k - 1)
                                if not (last and b):
                                    if u == 0 and (s, k) == (10, 2):
                                        split_weights(p + 1, 1 - b)
                                    if u in (1, 2) and (s, k) == (7, 1):
                                        table_far(p + 1, 1 - b, u - 1)
                                    if u in (1, 2) and (s, k) in ((9, 2), (11, 1)):
                                        table_side(1 - b, u - 1, (s - 9) // 2)
                                if (s, k) == (13, 2) and not final:
                                    combine(g + 1, nb, nu)
                                if (s, k) == (14, 2) and not final:
                                    rows(g + 1, nu)
                                if with_silu and (s, k) in silu_at:
                                    silu(l, silu_at.index((s, k)))
                    assert last or links[0] + (0 if first else 2 * NC) == body_links + 2 * NC, (links, body_links)
                loop(dve, body)
                for i in range(8):
                    ins = invert(NUNIT - 1, i)
                link(ins)
                normalise(NUNIT - 1, 1)
                accumulate(NUNIT - 1, NC - 1)


def finish(nc, x, silu_d, ident, sT, out):
    with ExitStack() as ctx:
        t_ = lambda name, shape, dt=F32: ctx.enter_context(nc.sbuf_tensor(name, shape, dt))
        s_ = lambda name: ctx.enter_context(nc.semaphore(name))
        ps = [ctx.enter_context(nc.psum_tensor(f"op{i}", [P, CH], F32)) for i in range(NC)]
        xt, gt, pt = t_("xt2", [P, NT, D]), t_("gt", [P, S]), t_("pt", [P, S])
        x_in, g_in = [s_(f"o_x{c}") for c in range(NC)], [s_(f"o_g{c}") for c in range(NC)]
        prod_ready, t_ready, o_ready, stored = s_("o_prod"), s_("o_t"), s_("o_sum"), s_("o_stored")
        xv = x.rearrange("o (t p) d -> p (o t) d", p=P)
        ov = out.rearrange("o (t p) d -> p (o t) d", p=P)
        with nc.Block() as block:
            @block.sync
            def _(sp):
                for c in range(NC):
                    sp.dma_start(gt[:, c * CH:(c + 1) * CH], silu_d[:, c * CH:(c + 1) * CH]).then_inc(g_in[c], 16)
                    sp.dma_start(xt[:, c * TC:(c + 1) * TC, :], xv[:, c * TC:(c + 1) * TC, :]).then_inc(x_in[c], 16)
                for c in range(NC):
                    sp.wait_ge(o_ready, c + 1)
                    sp.dma_start(ov[:, c * TC:(c + 1) * TC, :], xt[:, c * TC:(c + 1) * TC, :]).then_inc(stored, 16)
                sp.wait_ge(stored, 16 * NC)

            @block.vector
            def _(dve):
                for c in range(NC):
                    cs = slice(c * CH, (c + 1) * CH)
                    dve.wait_ge(g_in[c], 16)
                    nc.vector.tensor_tensor(pt[:, cs], sT[:, cs], gt[:, cs], ALU.mult).then_inc(prod_ready, 1)
                for c in range(NC):
                    dve.wait_ge(x_in[c], 16)
                    dve.wait_ge(t_ready, c + 1)
                    ts = slice(c * TC, (c + 1) * TC)
                    nc.vector.tensor_tensor(xt[:, ts, :], ps[c][:, :].rearrange("p (t d) -> p t d", t=TC), xt[:, ts, :],
                                            ALU.add).then_inc(o_ready, 1)

            @block.tensor
            def _(pe):
                for c in range(NC):
                    pe.wait_ge(prod_ready, c + 1)
                    for i in range(TC):
                        at = slice((c * TC + i) * P, (c * TC + i + 1) * P)
                        last = nc.tensor.transpose(ps[c][:, i * P:(i + 1) * P], pt[:, at], ident[:, :])
                    last.then_inc(t_ready, 1)


def build(nc, x, wq, wk, wv, wo, emb, wr, br, w1, b1, w2, b2, onehot, ident_c, mask_c, out):
    vec = nc.dram_tensor("bias_by_distance", [2, H, CH], F32, kind="Internal").ap()
    tabs = [nc.dram_tensor(f"bias_window{a}", [H, P, NEAR], F32, kind="Internal").ap() for a in range(2)]
    gates_d = nc.dram_tensor("gates", [E, S], F32, kind="Internal").ap()
    moe_d = nc.dram_tensor("moe", [D, S], F32, kind="Internal").ap()
    silu_d = nc.dram_tensor("silu", [D, S], F32, kind="Internal").ap()
    with ExitStack() as ctx:
        ident = ctx.enter_context(nc.sbuf_tensor("ident", [P, P], F32))
        sT = ctx.enter_context(nc.sbuf_tensor("sT", [P, S], F32))
        with nc.sbuf_tensor("xh", [P, S], F32R) as xh, nc.sbuf_tensor("xl", [P, S], F32R) as xl:
            prepare(nc, x, emb, onehot, ident_c, wr, br, xh, xl, ident, vec, tabs, gates_d)
            experts(nc, w1, b1, w2, b2, xh, xl, gates_d, moe_d)
            attention(nc, wq, wk, wv, wo, tabs, mask_c, xh, xl, ident, moe_d, silu_d, sT)
        finish(nc, x, silu_d, ident, sT, out)


_INS = ["L0_attn_hidden_states", "L0_attn_Wq", "L0_attn_Wk", "L0_attn_Wv", "L0_attn_Wo", "L0_attn_rel_bias_emb",
        "L0_ffn_Wr", "L0_ffn_br", "L0_ffn_W1", "L0_ffn_b1", "L0_ffn_W2", "L0_ffn_b2"]


def constants():
    import numpy as np
    starts = [0, 1, 2, 3, 4, 5, 6, 7, 8, 12, 16, 23, 32, 46, 64, 91]
    onehot = np.zeros((32, 2, 512), np.float32)
    for j in range(511):
        for a, rel in enumerate((255 - j, j - 255)):
            size = max(b for b in range(16) if starts[b] <= abs(rel))
            onehot[size + 16 * (rel > 0), a, j] = 1.0
    ident = np.eye(128, dtype=np.float32)
    mask = np.zeros((128, 16, 4), np.float32)
    for t in range(16):
        for c in range(4):
            mask[:, t, c] = float(t - 4 * c <= 1)
    return {"onehot": onehot, "ident": ident, "mask": mask}


def kernel(**inputs):
    import numpy as _np
    import concourse.bacc as _bacc
    from concourse import mybir as _mybir
    from concourse.bass_utils import run_bass_kernel_spmd as _run

    nc = _bacc.Bacc("TRN2", target_bir_lowering=False, num_devices=1)
    arrays, args = {}, []
    given = {n: inputs[n] for n in _INS}
    given.update(constants())
    for name, a in given.items():
        a = _np.ascontiguousarray(a)
        arrays[f"in_{name}"] = a
        args.append(nc.dram_tensor(f"in_{name}", a.shape, _mybir.dt.from_np(a.dtype), kind="ExternalInput").ap())
    args.append(nc.dram_tensor("out_0", (1, 2048, 128), _mybir.dt.float32, kind="ExternalOutput").ap())
    build(nc, *args)
    r = _run(nc, [arrays], core_ids=[0])
    return r.results[0]["out_0"]
```

```python
import concourse.bass as bass
from concourse import mybir
from contextlib import ExitStack

P = 128
S, D = 2048, 128
H, DK = 16, 64
NT = S // P
CH = 512
NC = S // CH
TC = CH // P
E, FF = 8, 512
NJ = FF // P
NPAIR = H // 2
NEAR = 3 * P
SAT = 91
BODY = 2 * NC
NUNIT = NPAIR * NC
NITER = NUNIT // BODY
RING = 8
EPS = 1e-5

F32, F32R, F16 = mybir.dt.float32, mybir.dt.float32r, mybir.dt.float16
ALU = mybir.AluOpType
ACT = mybir.ActivationFunctionType
AX = mybir.AxisListType.X


def need(eng, sem, value):
    if not isinstance(value, int) or value > 0:
        eng.wait_ge(sem, value)


def raw(ap):
    return ap.bitcast(F32)


class ExpertWeights:

    def __init__(self, nc, ctx):
        t_ = lambda name, shape, dt=F32: ctx.enter_context(nc.sbuf_tensor(name, shape, dt))
        s_ = lambda name: ctx.enter_context(nc.semaphore(name))
        self.w1r, self.w2r = t_("w1r", [P, 2, FF]), t_("w2r", [P, 2, NJ, D])
        self.w1h, self.w1l = t_("w1h", [P, 2, FF], F32R), t_("w1l", [P, 2, FF], F32R)
        self.w2h, self.w2l = t_("w2h", [P, 2, NJ * D], F32R), t_("w2l", [P, 2, NJ * D], F32R)
        self.b1s, self.b2s = t_("b1s", [P, 2, NJ]), t_("b2s", [P, 2, 1])
        self.loaded = [s_("f_loaded0"), s_("f_loaded1")]
        self.hi_split, self.split = s_("f_hi_split"), s_("f_split")

    def load(self, sp, b, e, w1, b1, w2, b2):
        done = self.loaded[b]
        sp.dma_start(self.w1r[:, b, :], w1[bass.ds(e, 1), :, :].rearrange("e d h -> d (e h)")).then_inc(done, 16)
        sp.dma_start(self.w2r[:, b, :, :], w2[bass.ds(e, 1), :, :].rearrange("e (j p) o -> p (e j) o", p=P)).then_inc(done, 16)
        sp.dma_start(self.b1s[:, b, :], b1[bass.ds(e, 1), :].rearrange("e (j p) -> p (e j)", p=P),
                     allow_slow_non_contiguous=True).then_inc(done, 16)
        sp.dma_start(self.b2s[:, b, :], b2[bass.ds(e, 1), :].rearrange("e p -> p e"),
                     allow_slow_non_contiguous=True).then_inc(done, 16)

    def high_parts(self, nc, b):
        nc.scalar.activation(self.w1h[:, b, :], self.w1r[:, b, :], ACT.Copy).then_inc(self.hi_split, 1)
        nc.scalar.activation(self.w2h[:, b, :], self.w2r[:, b, :, :].rearrange("p j o -> p (j o)"),
                             ACT.Copy).then_inc(self.hi_split, 1)

    def low_parts(self, nc, b):
        nc.gpsimd.tensor_tensor(self.w1l[:, b, :], self.w1r[:, b, :], raw(self.w1h[:, b, :]),
                                ALU.subtract).then_inc(self.split, 1)
        nc.gpsimd.tensor_tensor(self.w2l[:, b, :], self.w2r[:, b, :, :].rearrange("p j o -> p (j o)"),
                                raw(self.w2h[:, b, :]), ALU.subtract).then_inc(self.split, 1)


def prepare(nc, x, emb, onehot, ident_c, wr, br, xh, xl, ident, vec, tabs, gates_d, w1, b1, w2, b2, weights, g8, gates_stored,
            tabs_stored):
    with ExitStack() as ctx:
        t_ = lambda name, shape, dt=F32: ctx.enter_context(nc.sbuf_tensor(name, shape, dt))
        s_ = lambda name: ctx.enter_context(nc.semaphore(name))
        ps = [ctx.enter_context(nc.psum_tensor(f"pp{i}", [P, CH], F32)) for i in range(8)]
        xt, xn = t_("xt", [P, NT, D]), t_("xn", [P, NT, D])
        st, mv = t_("st", [P, NT, 6]), t_("mv", [P, NT, 2])
        va, sd, rs, t1, t2 = (t_(n, [P, NT]) for n in ("va", "sd", "rs", "t1", "t2"))
        emb_s, oh = t_("emb_s", [32, H]), t_("oh", [32, 2, CH])
        u_s = t_("u_s", [H, 2, CH])
        wr_s, wrh, wrl = t_("wr_s", [P, E]), t_("wrh", [P, P], F32R), t_("wrl", [P, P], F32R)
        lgT = t_("lgT", [E, S])
        br_s = t_("br_s", [P, E])
        lg, sel, cmp_, ex = (t_(n, [P, NT, E]) for n in ("lg", "sel", "cmp", "ex"))
        m1, z1 = t_("m1", [P, NT]), t_("z1", [P, NT])
        s_x, s_c = s_("a_x"), s_("a_const")
        var_ready, sd_ready, xn_ready = s_("a_var"), s_("a_sd"), s_("a_xn")
        xt_ready, xh_ready, xl_ready = s_("a_xt"), s_("a_xh"), s_("a_xl")
        u_ready, u_saved, wr_ready = s_("a_u"), s_("a_usaved"), s_("a_wr")
        lgT_ready, lgT_saved = s_("a_lgT"), s_("a_lgTsaved")
        lg_ready, mm_ready, ex_ready, gate_ready = s_("a_lg"), s_("a_shift"), s_("a_ex"), s_("a_gate")
        g8_ready, g8_saved, chain = s_("a_g8"), s_("a_g8saved"), s_("a_chain")
        vec_done = s_("a_vec")
        with nc.Block() as block:
            @block.sync
            def _(sp):
                sp.dma_start(xt[:, :, :], x.rearrange("o (t p) d -> p (o t) d", p=P)).then_inc(s_x, 16)
                sp.dma_start(emb_s[:, :], emb).then_inc(s_c, 16)
                sp.dma_start(oh[:, :, :], onehot).then_inc(s_c, 16)
                sp.dma_start(ident[:, :], ident_c).then_inc(s_c, 16)
                sp.dma_start(wr_s[:, :], wr).then_inc(s_c, 16)
                sp.dma_start(br_s[:, :], br.partition_broadcast(P)).then_inc(s_c, 16)
                weights.load(sp, 0, 0, w1, b1, w2, b2)
                sp.wait_ge(u_saved, 2)
                sp.dma_start(vec.rearrange("a h n -> h a n"), u_s[:, :, :]).then_inc(vec_done, 16)
                sp.wait_ge(vec_done, 16)
                for a in range(2):
                    window = bass.AP(tensor=vec.tensor, offset=a * H * CH + P - 1,
                                     ap=[[CH, H], [-1, P], [1, NEAR]])
                    sp.dma_start(tabs[a], window).then_inc(tabs_stored, 16)
                sp.wait_ge(g8_saved, NC)
                sp.dma_start(gates_d, g8[:, :]).then_inc(gates_stored, 16)

            @block.gpsimd
            def _(pool):
                pool.wait_ge(weights.hi_split, 2)
                weights.low_parts(nc, 0)

            @block.vector
            def _(dve):
                done = [0]

                def link(ins):
                    done[0] += 1
                    ins.then_inc(chain, 1)
                    dve.wait_ge(chain, done[0])

                nc.vector.memset(raw(wrh[:, :]), 0.0)
                link(nc.vector.memset(raw(wrl[:, :]), 0.0))
                dve.wait_ge(s_c, 80)
                link(nc.vector.tensor_copy(wrh[:, 0:E], wr_s[:, :]))
                nc.vector.tensor_tensor(wrl[:, 0:E], wr_s[:, :], raw(wrh[:, 0:E]), ALU.subtract).then_inc(wr_ready, 1)
                dve.wait_ge(s_x, 16)
                for t in range(NT):
                    last = nc.vector.bn_stats(st[:, t, :], xt[:, t, :])
                link(last)
                for t in range(NT):
                    last = nc.vector.bn_aggr(mv[:, t, :], st[:, t, :])
                link(last)
                nc.vector.tensor_scalar(va[:, :], mv[:, :, 1], EPS, None, ALU.add).then_inc(var_ready, 1)
                dve.wait_ge(sd_ready, 1)
                link(nc.vector.reciprocal(rs[:, :], sd[:, :]))
                link(nc.vector.tensor_tensor(t1[:, :], rs[:, :], rs[:, :], ALU.mult))
                link(nc.vector.tensor_tensor(t2[:, :], t1[:, :], va[:, :], ALU.mult))
                link(nc.vector.tensor_scalar(t1[:, :], t2[:, :], -0.5, 1.5, ALU.mult, ALU.add))
                link(nc.vector.tensor_tensor(sd[:, :], rs[:, :], t1[:, :], ALU.mult))
                for t in range(NT):
                    nc.vector.tensor_scalar(xn[:, t, :], xt[:, t, :], mv[:, t, 0:1], sd[:, t:t + 1],
                                            ALU.subtract, ALU.mult).then_inc(xn_ready, 1)
                for c in range(NC):
                    dve.wait_ge(xh_ready, c + 1)
                    nc.vector.tensor_tensor(xl[:, c * CH:(c + 1) * CH], ps[c][:, :],
                                            raw(xh[:, c * CH:(c + 1) * CH]), ALU.subtract).then_inc(xl_ready, 1)
                dve.wait_ge(u_ready, 1)
                for a in range(2):
                    nc.vector.tensor_copy(u_s[:, a, :], ps[4 + a][0:H, :]).then_inc(u_saved, 1)
                for c in range(NC):
                    dve.wait_ge(lgT_ready, c + 1)
                    nc.vector.tensor_copy(lgT[:, c * CH:(c + 1) * CH], ps[c][0:E, :]).then_inc(lgT_saved, 1)
                dve.wait_ge(lg_ready, 1)
                link(nc.vector.tensor_tensor(lg[:, :, :], ps[6][:, 0:NT * E].rearrange("p (t e) -> p t e", e=E),
                                             br_s[:, :].unsqueeze(1).to_broadcast([P, NT, E]), ALU.add))
                link(nc.vector.reduce_max(m1[:, :], lg[:, :, :], AX))
                link(nc.vector.tensor_tensor(ex[:, :, :], lg[:, :, :],
                                             m1[:, :].unsqueeze(2).to_broadcast([P, NT, E]), ALU.subtract))
                nc.vector.memset(sel[:, :, :], 0.0).then_inc(mm_ready, 1)
                for o in range(E):
                    for lo, hi, op in ((0, o, ALU.is_gt), (o, E, ALU.is_ge)):
                        if hi > lo:
                            other = lg[:, :, o:o + 1].to_broadcast([P, NT, hi - lo])
                            last = nc.vector.tensor_tensor(cmp_[:, :, lo:hi], other, lg[:, :, lo:hi], op)
                    link(last)
                    link(nc.vector.tensor_tensor(sel[:, :, :], sel[:, :, :], cmp_[:, :, :], ALU.add))
                link(nc.vector.tensor_scalar(sel[:, :, :], sel[:, :, :], 2.5, None, ALU.is_lt))
                dve.wait_ge(ex_ready, 1)
                link(nc.vector.tensor_tensor(ex[:, :, :], ex[:, :, :], sel[:, :, :], ALU.mult))
                link(nc.vector.reduce_sum(z1[:, :], ex[:, :, :], AX))
                link(nc.vector.reciprocal(m1[:, :], z1[:, :]))
                nc.vector.tensor_tensor(sel[:, :, :], ex[:, :, :],
                                        m1[:, :].unsqueeze(2).to_broadcast([P, NT, E]), ALU.mult).then_inc(gate_ready, 1)
                for c in range(NC):
                    dve.wait_ge(g8_ready, c + 1)
                    nc.vector.tensor_copy(g8[:, c * CH:(c + 1) * CH], ps[c][0:E, :]).then_inc(g8_saved, 1)

            @block.scalar
            def _(act):
                act.wait_ge(var_ready, 1)
                nc.scalar.activation(sd[:, :], va[:, :], ACT.Sqrt).then_inc(sd_ready, 1)
                for c in range(NC):
                    act.wait_ge(xt_ready, c + 1)
                    nc.scalar.activation(xh[:, c * CH:(c + 1) * CH], ps[c][:, :], ACT.Copy).then_inc(xh_ready, 1)
                act.wait_ge(weights.loaded[0], 64)
                weights.high_parts(nc, 0)
                act.wait_ge(mm_ready, 1)
                nc.scalar.activation(ex[:, :, :], ex[:, :, :], ACT.Exp).then_inc(ex_ready, 1)

            @block.tensor
            def _(pe):
                pe.wait_ge(s_c, 80)
                for a in range(2):
                    last = nc.tensor.matmul(ps[4 + a][0:H, :], emb_s[:, :], oh[:, a, :], start=True, stop=True)
                last.then_inc(u_ready, 1)
                for c in range(NC):
                    pe.wait_ge(xn_ready, (c + 1) * TC)
                    for i in range(TC):
                        last = nc.tensor.transpose(ps[c][:, i * P:(i + 1) * P], xn[:, c * TC + i, :], ident[:, :])
                    last.then_inc(xt_ready, 1)
                pe.wait_ge(wr_ready, 1)
                for c in range(NC):
                    pe.wait_ge(xl_ready, c + 1)
                    parts = [(a, b) for a in (wrh, wrl) for b in (xh, xl)]
                    for n, (a, b) in enumerate(parts):
                        last = nc.tensor.matmul(ps[c][:, :], a[:, :], b[:, c * CH:(c + 1) * CH], start=n == 0, stop=n == 3)
                    last.then_inc(lgT_ready, 1)
                for t in range(NT):
                    pe.wait_ge(lgT_saved, t // TC + 1)
                    last = nc.tensor.transpose(ps[6][:, t * E:(t + 1) * E], lgT[:, t * P:(t + 1) * P], ident[0:E, 0:E])
                last.then_inc(lg_ready, 1)
                pe.wait_ge(gate_ready, 1)
                for c in range(NC):
                    for i in range(TC):
                        last = nc.tensor.transpose(ps[c][0:E, i * P:(i + 1) * P], sel[:, c * TC + i, :], ident[:, :])
                    last.then_inc(g8_ready, 1)


def experts(nc, w1, b1, w2, b2, xh, xl, gates_d, gates_stored, sT, wq, wk, wv, weights, first_pair):
    WR, WH, WL, w_loaded, wh_ready, wl_ready = first_pair
    w1h, w1l, w2h, w2l, b1s, b2s = weights.w1h, weights.w1l, weights.w2h, weights.w2l, weights.b1s, weights.b2s
    loaded, hi_split, split = weights.loaded, weights.hi_split, weights.split
    with ExitStack() as ctx:
        t_ = lambda name, shape, dt=F32: ctx.enter_context(nc.sbuf_tensor(name, shape, dt))
        s_ = lambda name: ctx.enter_context(nc.semaphore(name))
        hp = [ctx.enter_context(nc.psum_tensor(f"hp{i}", [P, CH], F32)) for i in range(NJ)]
        yp = [ctx.enter_context(nc.psum_tensor(f"yp{i}", [P, CH], F32)) for i in range(2)]
        gb = t_("gb", [P, 2, S])
        h32 = t_("h32", [P, 2, NJ, CH])
        hh, hl = t_("hh", [P, 2, NJ, CH], F32R), t_("hl", [P, 2, NJ, CH], F32R)
        yg = t_("yg", [P, 2, CH])
        gload = [s_("f_gload0"), s_("f_gload1")]
        hp_ready, h32_ready, h_ready, yp_ready = s_("f_hp"), s_("f_h32"), s_("f_h"), s_("f_yp")
        hh_ready, yg_ready, sum_done = s_("f_hh"), s_("f_yg"), s_("f_sum")
        bodies = 2 * NC

        def loop(eng, body):
            body(0, True, False)
            with eng.Fori(1, E // 2 - 1) as it:
                body(it, False, False)
            body(E // 2 - 1, False, True)

        with nc.Block() as block:
            @block.sync
            def _(sp):
                def body(it, first, last):
                    for b in range(2):
                        e = it * 2 + b
                        if first and b:
                            for n, w in enumerate((wq, wk, wv)):
                                sp.dma_start(WR[:, n * P:(n + 1) * P], w[:, 0:P]).then_inc(w_loaded, 16)
                        need(sp, yg_ready, (e - 1) * NC)
                        if b or not first:
                            weights.load(sp, b, e, w1, b1, w2, b2)
                        if first and b == 0:
                            sp.wait_ge(gates_stored, 16)
                        g = bass.AP(tensor=gates_d.tensor, offset=e * S, ap=[[0, P], [1, S]])
                        sp.dma_start(gb[:, b, :], g).then_inc(gload[b], 16)
                loop(sp, body)

            @block.gpsimd
            def _(pool):
                nc.gpsimd.memset(sT[:, :], 0.0).then_inc(sum_done, 1)

                def add(n, c):
                    pool.wait_ge(yg_ready, n + 1)
                    pool.wait_ge(sum_done, n + 1)
                    nc.gpsimd.tensor_tensor(sT[:, c * CH:(c + 1) * CH], sT[:, c * CH:(c + 1) * CH],
                                            yg[:, c % 2, :], ALU.add).then_inc(sum_done, 1)

                def body(it, first, last):
                    for b in range(2):
                        e = it * 2 + b
                        need(pool, yp_ready, (e - 1) * NC)
                        if b or not first:
                            pool.wait_ge(hi_split, e * 2 + 2)
                            weights.low_parts(nc, b)
                        for c in range(NC):
                            if not (first and b == 0):
                                add((e - 1) * NC + c, c)
                loop(pool, body)
                pool.wait_ge(wh_ready, 1)
                nc.gpsimd.tensor_tensor(WL[:, 0, :], WR[:, :], raw(WH[:, 0, :]), ALU.subtract).then_inc(wl_ready, 1)
                for c in range(NC):
                    add((E - 1) * NC + c, c)

            @block.tensor
            def _(pe):
                def up(it, b, c):
                    e = it * 2 + b
                    n = e * NC + c
                    if c == 0:
                        pe.wait_ge(split, e * 2 + 1)
                    for j in range(NJ):
                        need(pe, h32_ready, (n - 1) * NJ + j + 1)
                        w = slice(j * P, (j + 1) * P)
                        xs = slice(c * CH, (c + 1) * CH)
                        nc.tensor.matmul(hp[j][:, :], w1h[:, b, w], xh[:, xs], start=True, stop=False)
                        nc.tensor.matmul(hp[j][:, :], w1l[:, b, w], xh[:, xs], start=False, stop=False)
                        nc.tensor.matmul(hp[j][:, :], w1h[:, b, w], xl[:, xs], start=False, stop=True).then_inc(hp_ready, 1)

                def down(it, b, c):
                    n = (it * 2 + b) * NC + c
                    if c == 0:
                        pe.wait_ge(split, (it * 2 + b) * 2 + 2)
                    need(pe, yg_ready, n - 1)
                    for j in range(NJ):
                        pe.wait_ge(h_ready, n * NJ + j + 1)
                        w = slice(j * P, (j + 1) * P)
                        nc.tensor.matmul(yp[c % 2][:, :], w2h[:, b, w], hh[:, c % 2, j, :], start=j == 0, stop=False)
                        nc.tensor.matmul(yp[c % 2][:, :], w2l[:, b, w], hh[:, c % 2, j, :], start=False, stop=False)
                        last = nc.tensor.matmul(yp[c % 2][:, :], w2h[:, b, w], hl[:, c % 2, j, :], start=False, stop=j == NJ - 1)
                    last.then_inc(yp_ready, 1)

                def body(it, first, last):
                    for b in range(2):
                        for c in range(NC):
                            up(it, b, c)
                            if c:
                                down(it, b, c - 1)
                            elif b:
                                down(it, 0, NC - 1)
                            elif not first:
                                down(it - 1, 1, NC - 1)
                loop(pe, body)
                down(E // 2 - 1, 1, NC - 1)

            @block.scalar
            def _(act):
                def split_high(it, b):
                    act.wait_ge(loaded[b], (it + 1) * 64)
                    need(act, yp_ready, (it * 2 + b - 1) * NC)
                    weights.high_parts(nc, b)

                def body(it, first, last):
                    for b in range(2):
                        e = it * 2 + b
                        for c in range(NC):
                            if c == 2 and not (last and b):
                                split_high(it + b, 1 - b)
                            n = e * NC + c
                            for j in range(NJ):
                                act.wait_ge(hp_ready, n * NJ + j + 1)
                                need(act, h_ready, (n - 2) * NJ + j + 1)
                                nc.scalar.activation(h32[:, c % 2, j, :], hp[j][:, :], ACT.Relu,
                                                     bias=b1s[:, b, j:j + 1]).then_inc(h32_ready, 1)
                        if first and b == 0:
                            act.wait_ge(w_loaded, 48)
                            nc.scalar.activation(WH[:, 0, :], WR[:, :], ACT.Copy).then_inc(wh_ready, 1)
                loop(act, body)

            @block.vector
            def _(dve):
                def halves(it, b, c):
                    n = (it * 2 + b) * NC + c
                    for j in range(NJ):
                        dve.wait_ge(h32_ready, n * NJ + j + 1)
                        if j == 0:
                            need(dve, yp_ready, n - 1)
                        nc.vector.tensor_copy(hh[:, c % 2, j, :], h32[:, c % 2, j, :]).then_inc(hh_ready, 1)
                        dve.wait_ge(hh_ready, n * NJ + j + 1)
                        nc.vector.tensor_tensor(hl[:, c % 2, j, :], h32[:, c % 2, j, :],
                                                raw(hh[:, c % 2, j, :]), ALU.subtract).then_inc(h_ready, 1)

                def gated(it, b, c):
                    e = it * 2 + b
                    n = e * NC + c
                    if c == 0:
                        dve.wait_ge(gload[b], (it + 1) * 16)
                        dve.wait_ge(loaded[b], (it + 1) * 64)
                    dve.wait_ge(yp_ready, n + 1)
                    need(dve, sum_done, n)
                    nc.vector.scalar_tensor_tensor(out=yg[:, c % 2, :], in0=yp[c % 2][:, :], scalar=b2s[:, b, 0:1],
                                                   in1=gb[:, b, c * CH:(c + 1) * CH], op0=ALU.add,
                                                   op1=ALU.mult).then_inc(yg_ready, 1)

                def body(it, first, last):
                    for b in range(2):
                        for c in range(NC):
                            halves(it, b, c)
                            if c:
                                gated(it, b, c - 1)
                            elif b:
                                gated(it, 0, NC - 1)
                            elif not first:
                                gated(it - 1, 1, NC - 1)
                loop(dve, body)
                gated(E // 2 - 1, 1, NC - 1)


def near_columns(r):
    start = (r - 1) * P
    lo = max(start if r <= 1 else start + P - SAT + 1, 0)
    hi = min(start + 2 * P + SAT - 1 if r <= 1 else start + NEAR, CH)
    return slice(lo, hi), slice(lo - start, hi - start)


def chunks_of(s):
    full = 2 * TC * NC
    return list(range(min(s * full // 13, full), min((s + 1) * full // 13, full)))


def attention(nc, wq, wk, wv, wo, tabs, mask_c, xh, xl, ident, sT, tabs_stored, silu_d, x, out, first_pair):
    WR, WH, WL, w_loaded, wh_ready, wl_ready = first_pair
    with ExitStack() as ctx:
        t_ = lambda name, shape, dt=F32: ctx.enter_context(nc.sbuf_tensor(name, shape, dt))
        s_ = lambda name: ctx.enter_context(nc.semaphore(name))
        bank = lambda name: ctx.enter_context(nc.psum_tensor(name, [P, CH], F32))
        SM = [bank("SM0"), bank("SM1")]
        ST = [bank("ST0"), bank("ST1")]
        CT = [bank("CT0"), bank("CT1")]
        MV = bank("MV")
        MP = bank("MP")
        Q1 = [t_(f"Q1{h}", [P, S], F32R) for h in range(2)]
        Q2 = [t_(f"Q2{h}", [P, S], F32R) for h in range(2)]
        K1 = [[t_(f"K1{b}{h}", [P, S], F32R) for h in range(2)] for b in range(2)]
        K2 = [[t_(f"K2{b}{h}", [P, S], F32R) for h in range(2)] for b in range(2)]
        V = [t_(f"V{b}", [P, NT, 2 * DK]) for b in range(2)]
        PR = t_("PR", [P, RING, CH])
        Z = t_("Z", [P, 2, 2, CH])
        rz = t_("rz", [P, CH])
        TR = t_("TR", [P, 2, NEAR])
        TH = t_("TH", [P, 2, 2, 2, NEAR], F32R)
        TL = t_("TL", [P, 2, 2, 2, NEAR], F16)
        TM = t_("TM", [P, 2, 2, 2, NEAR], F32R)
        far = t_("far", [P, 2, 2, 2])
        fd = t_("fd", [P, 2])
        fm = t_("fm", [P, 2, 2, NT, NC])
        WO = t_("WO", [P, 2, D])
        identr, ident16 = t_("identr", [P, P], F32R), t_("ident16", [P, P], F16)
        ones = t_("ones", [P, DK])
        mask = t_("mask", [P, NT, NC])
        mx, mxb, nm = t_("mx", [P, 2, TC, NC]), t_("mxb", [P, 2, TC, NC]), t_("nm", [P, 2, TC])

        t_loaded, c_loaded = s_("t_loaded"), s_("c_loaded")
        wo_loaded = [s_("wo_loaded0"), s_("wo_loaded1")]
        q_copied = [s_("q_copied0"), s_("q_copied1")]
        k_copied = [s_("k_copied0"), s_("k_copied1")]
        const_ready, tab_ready = s_("const_ready"), s_("tab_ready")
        mp_ready, hi_ready, mp_free = s_("mp_ready"), s_("hi_ready"), s_("mp_free")
        sm_ready, mx_ready, nm_ready = s_("sm_ready"), s_("mx_ready"), s_("nm_ready")
        mt_ready, rows_ready = s_("mt_ready"), s_("rows_ready")
        st_ready, exp_ready, pv_done, z_done = s_("st_ready"), s_("exp_ready"), s_("pv_done"), s_("z_done")
        z1_done = s_("z1_done")
        zb_ready, ctx_ready, wo_ready, sum_ready = s_("zb_ready"), s_("ctx_ready"), s_("wo_ready"), s_("sum_ready")
        chain = s_("dve_chain")
        silu_b = V[0][:, :, :].rearrange("p t d -> p (t d)")
        x_b = TR[:, :, :].rearrange("p a n -> p (a n)")[:, 0:CH].rearrange("p (t d) -> p t d", t=TC)
        x_tiles, out_tiles = (a.rearrange("o (t p) d -> p (o t) d", p=P) for a in (x, out))
        silu_back, x_back = s_("silu_back"), s_("x_back")
        gated_ready, back_ready, out_ready, out_stored = s_("gated_ready"), s_("back_ready"), s_("out_ready"), s_("out_stored")
        moe_exp, silu_ready, silu_stored = s_("moe_exp"), s_("silu_ready"), s_("silu_stored")

        job_list = {u: [("q", 5, 0), ("kkvv"[u], 9, 2 * (u % 2)), ("kkvv"[u], 15, 2 * (u % 2) + 1)] for u in range(NC)}
        start_jobs = [("q", 0)] + [("k", c) for c in range(NC)] + [("q", 1)] + [("v", c) for c in range(NC)]

        start_banks = [ST[0], ST[1], MP, MV, CT[1]]
        start_maxima = [SM[0], SM[1], CT[0]]

        def jobs_of(l, last):
            return [(kind, slot, c) for kind, slot, c in job_list[l % NC]
                    if not (last and (l >= NC and kind != "q" or l + 2 >= BODY))]

        def jobs_before(l, last=False):
            full = [kind for m in range(l) for kind, _, _ in jobs_of(m, last)]
            return len(full), sum(kind != "v" for kind in full)

        JOBS, HIGHS = jobs_before(BODY)

        def jobs(it, l, last):
            n, m = jobs_before(l, last)
            n, m = n + 10 + it * JOBS, m + 6 + it * HIGHS
            out = []
            for kind, slot, c in jobs_of(l, last):
                out.append((kind, slot, c, n, m))
                n, m = n + 1, m + (kind != "v")
            return out

        def loop(eng, body):
            body(0, True, False)
            with eng.Fori(1, NITER - 1) as it:
                body(it, False, False)
            body(NITER - 1, False, True)

        with nc.Block() as block:
            @block.sync
            def _(sp):
                sp.dma_start(mask[:, :, :], mask_c).then_inc(c_loaded, 16)

                def weights(p):
                    cols = bass.ds(p * P, P)
                    for n, w in enumerate((wq, wk, wv)):
                        sp.dma_start(WR[:, n * P:(n + 1) * P], w[:, cols]).then_inc(w_loaded, 16)

                def table(p, h):
                    for a in range(2):
                        sp.dma_start(TR[:, a, :], tabs[a][bass.ds(p * 2 + h, 1), :, :].rearrange("h p n -> p (h n)")
                                     ).then_inc(t_loaded, 16)

                def load_wo(p, b):
                    sp.dma_start(WO[:, b, :], wo[bass.ds(p * P, P), :]).then_inc(wo_loaded[b], 16)

                def copy_q(u, m):
                    sp.wait_ge(hi_ready, m + 1)
                    for h in range(2):
                        cs = slice(u * CH, (u + 1) * CH)
                        sp.dma_start(raw(Q1[h][DK:P, cs]), raw(Q1[h][0:DK, cs])).then_inc(q_copied[u % 2], 16)

                def copy_k(b, c, m):
                    sp.wait_ge(hi_ready, m + 1)
                    for h in range(2):
                        cs = slice(c * CH, (c + 1) * CH)
                        sp.dma_start(raw(K2[b][h][0:DK, cs]), raw(K1[b][h][0:DK, cs])).then_inc(k_copied[b], 16)

                sp.wait_ge(tabs_stored, 32)
                table(0, 0)
                load_wo(0, 0)
                copy_q(0, 0)
                sp.wait_ge(tab_ready, 1)
                table(0, 1)
                for c in range(NC):
                    copy_k(0, c, 1 + c)
                copy_q(1, 1 + NC)

                def load_x(c):
                    need(sp, out_stored, 16 * c)
                    sp.dma_start(x_b, x_tiles[:, c * TC:(c + 1) * TC, :]).then_inc(x_back, 16)

                def store(c):
                    sp.wait_ge(out_ready, c + 1)
                    sp.dma_start(out_tiles[:, c * TC:(c + 1) * TC, :], x_b).then_inc(out_stored, 16)

                def body(it, first, last):
                    for l in range(BODY):
                        b, u = l // NC, l % NC
                        p = it * 2 + b
                        more = not (last and b)
                        if u == 0 and more:
                            sp.wait_ge(wl_ready, p + 1)
                            weights(p + 1)
                            sp.wait_ge(tab_ready, p * 2 + 2)
                            table(p + 1, 0)
                        if u == 1 and more:
                            sp.wait_ge(wo_ready, it * BODY + l - 1)
                            load_wo(p + 1, 1 - b)
                        if u == 2 and more:
                            sp.wait_ge(tab_ready, p * 2 + 3)
                            table(p + 1, 1)
                        if last and l == NC:
                            sp.wait_ge(tab_ready, 2 * NPAIR)
                            load_x(0)
                            sp.wait_ge(pv_done, (it * BODY + NC) * NT)
                            sp.wait_ge(silu_stored, 16 * NC)
                            sp.dma_start(silu_b, silu_d).then_inc(silu_back, 16)
                        for kind, _, c, _, m in jobs(it, l, last):
                            if kind == "k":
                                copy_k(1 - b, c, m)
                            elif kind == "q":
                                copy_q((u + 2) % NC, m)
                        if first and l < NC:
                            sp.wait_ge(silu_ready, l + 1)
                            sp.dma_start(silu_d[:, u * CH:(u + 1) * CH], rz[:, :]).then_inc(silu_stored, 16)
                        if last and l > NC:
                            store(l - NC - 1)
                            load_x(l - NC)
                loop(sp, body)
                store(NC - 1)
                sp.wait_ge(out_stored, 16 * NC)

            @block.gpsimd
            def _(pool):
                nc.gpsimd.memset(ones[:, :], 1.0).then_inc(const_ready, 1)
                for b in range(2):
                    for h in range(2):
                        pool.wait_ge(const_ready, 1 + 2 * b + h)
                        nc.gpsimd.memset(raw(K2[b][h][DK:DK + TC, :]), 1.0).then_inc(const_ready, 1)

                def body(it, first, last):
                    for l in range(BODY):
                        g = it * BODY + l
                        heads = 1 if last and l == BODY - 1 else 2
                        z = Z[:, l % 2, 0:heads, :]
                        tile = lambda k: PR[:, 2 * k % RING:2 * k % RING + heads, :]
                        for s in range(1, NT):
                            pool.wait_ge(exp_ready, g * 2 * NT + 2 * s + 2)
                            if s == 1:
                                need(pool, zb_ready, g - 1)
                                a = tile(0)
                            else:
                                pool.wait_ge(z_done, g * (NT - 1) + s - 1)
                                a = z
                            nc.gpsimd.tensor_tensor(z, a, tile(s), ALU.add).then_inc(z_done, 1)
                loop(pool, body)

            @block.tensor
            def _(pe):
                def split_product(out, a, b, first=True, last=True):
                    nc.tensor.matmul(out, a[0], b[0], start=first, stop=False)
                    nc.tensor.matmul(out, a[1], b[0], start=False, stop=False)
                    return nc.tensor.matmul(out, a[0], b[1], start=False, stop=last)

                def project(kind, b, c, n, out=MP, behind=1):
                    need(pe, mp_free, n - behind + 1)
                    if kind == "v":
                        w = slice(2 * P, 3 * P)
                        for i in range(TC):
                            xs = slice((c * TC + i) * P, (c * TC + i + 1) * P)
                            last = split_product(out[:, i * P:(i + 1) * P], (xh[:, xs], xl[:, xs]),
                                                 (WH[:, b, w], WL[:, b, w]))
                    else:
                        w = slice(0, P) if kind == "q" else slice(P, 2 * P)
                        xs = slice(c * CH, (c + 1) * CH)
                        last = split_product(out[:, :], (WH[:, b, w], WL[:, b, w]), (xh[:, xs], xl[:, xs]))
                    last.then_inc(mp_ready, 1)

                def maxima(n0, b, u, m, banks=SM):
                    h, t, c = m // (TC * NC), m // NC % TC, m % NC
                    need(pe, mx_ready, n0 + m - len(banks) + 1)
                    T = u * TC + t
                    out = banks[m % len(banks)]
                    r = T - c * TC
                    near = -1 <= r <= TC
                    last = nc.tensor.matmul(out[:, :], Q1[h][:, T * P:(T + 1) * P], K1[b][h][:, c * CH:(c + 1) * CH],
                                            start=True, stop=not near)
                    if near:
                        cols, of_table = near_columns(r)
                        last = nc.tensor.matmul(out[:, cols], identr[:, :], TM[:, b, h, int(r <= 1), of_table],
                                                start=False, stop=True)
                    last.then_inc(sm_ready, 1)

                def ready_for_maxima(p, u, g, n_job):
                    pe.wait_ge(mp_free, n_job + 1)
                    pe.wait_ge(q_copied[u % 2], (p * 2 + u // 2 + 1) * 32)
                    if u == 0:
                        pe.wait_ge(tab_ready, p * 2 + 2)

                def turn(g):
                    pe.wait_ge(nm_ready, g + 1)
                    need(pe, sum_ready, g - 1)
                    for h in range(2):
                        last = nc.tensor.transpose(MV[0:TC, h * P:(h + 1) * P], nm[:, h, :], ident[:, :])
                    last.then_inc(mt_ready, 1)

                def scores(g, b, u, s, h):
                    need(pe, exp_ready, g * 2 * NT + 2 * s + h - 1)
                    ks, qs = slice(s * P, (s + 1) * P), slice(u * CH, (u + 1) * CH)
                    r = s - u * TC
                    near = -1 <= r <= TC
                    nc.tensor.matmul(ST[h][:, :], K1[b][h][:, ks], Q1[h][:, qs], start=True, stop=False)
                    last = nc.tensor.matmul(ST[h][:, :], K2[b][h][0:DK + TC, ks], Q2[h][0:DK + TC, qs],
                                            start=False, stop=not near)
                    if near:
                        side, (cols, of_table) = int(r > 1), near_columns(r)
                        nc.tensor.matmul(ST[h][:, cols], identr[:, :], TH[:, b, h, side, of_table],
                                         start=False, stop=False)
                        last = nc.tensor.matmul(ST[h][:, cols], ident16[:, :], TL[:, b, h, side, of_table],
                                                start=False, stop=True)
                    last.then_inc(st_ready, 1)

                def values(g, b, par, s, after_silu=False):
                    pe.wait_ge(exp_ready, g * 2 * NT + 2 * s + 2)
                    if s == 0:
                        need(pe, ctx_ready, g - 1)
                        if after_silu:
                            pe.wait_ge(silu_ready, g)
                    for h in range(2):
                        rows = slice(h * DK, (h + 1) * DK)
                        last = nc.tensor.matmul(CT[par][rows, :], V[b][:, s, rows], PR[:, (2 * s + h) % RING, :],
                                                start=s == 0, stop=s == NT - 1)
                    last.then_inc(pv_done, 1)

                def sums(g, par):
                    pe.wait_ge(z_done, (g + 1) * (NT - 1))
                    pe.wait_ge(rows_ready, g + 1)
                    for h in range(2):
                        if h and isinstance(g, int) and g == NUNIT - 1:
                            pe.wait_ge(z1_done, NT - 1)
                        last = nc.tensor.matmul(MV[h * DK:(h + 1) * DK, :], ones[:, :], Z[:, par, h, :],
                                                start=True, stop=True)
                    last.then_inc(zb_ready, 1)

                def output(g, b, it):
                    pe.wait_ge(ctx_ready, g + 1)
                    pe.wait_ge(wo_loaded[b], (it + 1) * 16)
                    nc.tensor.matmul(MV[:, :], WO[:, b, :], rz[:, :], start=True, stop=True).then_inc(wo_ready, 1)

                def turn_back(c):
                    pe.wait_ge(gated_ready, c + 1)
                    if c:
                        pe.wait_ge(out_ready, c)
                    else:
                        pe.wait_ge(mp_free, 10 + (NITER - 1) * JOBS + jobs_before(BODY, True)[0])
                    for i in range(TC):
                        at = slice((c * TC + i) * P, (c * TC + i + 1) * P)
                        ins = nc.tensor.transpose(MP[:, i * P:(i + 1) * P], silu_b[:, at], ident[:, :])
                    ins.then_inc(back_ready, 1)

                pe.wait_ge(wl_ready, 1)
                for n, (kind, c) in enumerate(start_jobs):
                    project(kind, 0, c, n, start_banks[n % 5], 5)
                pe.wait_ge(mp_free, 1 + NC)
                pe.wait_ge(q_copied[0], 32)
                for m in range(2 * TC * NC):
                    if m % (TC * NC) == 0:
                        pe.wait_ge(tab_ready, m // (TC * NC) + 1)
                    maxima(0, 0, 0, m, start_maxima)
                pe.wait_ge(mp_free, 10)
                turn(0)

                def body(it, first, last):
                    for l in range(BODY):
                        b, u = l // NC, l % NC
                        g, p = it * BODY + l, it * 2 + b
                        nb, nu = (l + 1) % BODY // NC, (l + 1) % NC
                        lb, lit = ((l - 1) % BODY) // NC, it if l else it - 1
                        final = last and l == BODY - 1
                        todo = {slot: (kind, c, n) for kind, slot, c, n, _ in jobs(it, l, last)}
                        pe.wait_ge(rows_ready, g + 1)
                        if u == 0:
                            pe.wait_ge(k_copied[b], (it + 1) * 32 * NC)
                        if not final:
                            q_job = jobs(it, l - 1, last)[0][3] if l else it * JOBS + 10 - len(job_list[NC - 1])
                            ready_for_maxima(it * 2 + (l + 1) // NC, nu, g + 1, q_job)
                        for s in range(NT):
                            chunks = [] if final else chunks_of(s)
                            for h in range(2):
                                scores(g, b, u, s, h)
                                for m in chunks[h:h + 1]:
                                    maxima((g + 1) * 2 * TC * NC, nb, nu, m)
                            if s:
                                values(g, b, l % 2, s - 1, first and 1 <= l <= NC)
                            elif not (first and l == 0):
                                values(g - 1, lb, (l - 1) % 2, NT - 1)
                            for m in chunks[2:]:
                                maxima((g + 1) * 2 * TC * NC, nb, nu, m)
                            if s == 14 and not final:
                                turn(g + 1)
                            if not (first and l == 0):
                                if s == 2:
                                    sums(g - 1, (l - 1) % 2)
                                if s == 8:
                                    output(g - 1, lb, lit)
                            if last and l > NC and s == 12:
                                turn_back(l - NC - 1)
                            if s in todo:
                                kind, c, n = todo[s]
                                if kind == "q":
                                    project("q", (l + 2) % BODY // NC, (u + 2) % NC, n)
                                else:
                                    project(kind, 1 - b, c, n)
                loop(pe, body)
                values(NUNIT - 1, 1, 1, NT - 1)
                pe.wait_ge(sum_ready, NUNIT - 1)
                sums(NUNIT - 1, 1)
                output(NUNIT - 1, 1, NITER - 1)
                turn_back(NC - 1)

            @block.scalar
            def _(act):
                def split_weights(p, b):
                    act.wait_ge(w_loaded, (p + 1) * 48)
                    nc.scalar.activation(WH[:, b, :], WR[:, :], ACT.Copy).then_inc(wh_ready, 1)

                def high(kind, b, c, n, src=MP):
                    act.wait_ge(mp_ready, n + 1)
                    for h in range(2):
                        dst = Q1[h] if kind == "q" else K1[b][h]
                        last = nc.scalar.activation(dst[0:DK, c * CH:(c + 1) * CH], src[h * DK:(h + 1) * DK, :], ACT.Copy)
                    last.then_inc(hi_ready, 1)

                for n, (kind, c) in enumerate(start_jobs):
                    if kind != "v":
                        high(kind, 0, c, n, start_banks[n % 5])
                    else:
                        if c == 0:
                            act.wait_ge(mp_free, n)
                        act.wait_ge(mp_ready, n + 1)
                        nc.scalar.activation(V[0][:, c * TC:(c + 1) * TC, :],
                                             start_banks[n % 5][:, :].rearrange("p (t d) -> p t d", t=TC),
                                             ACT.Copy).then_inc(mp_free, 1)

                def body(it, first, last):
                    for l in range(BODY):
                        b, u = l // NC, l % NC
                        g, p = it * BODY + l, it * 2 + b
                        todo = {slot: (kind, c, n) for kind, slot, c, n, _ in jobs(it, l, last)}
                        if u == 0:
                            act.wait_ge(tab_ready, p * 2 + 2)
                        for s in range(NT):
                            for h in range(2):
                                n = g * 2 * NT + 2 * s + h
                                act.wait_ge(st_ready, n + 1)
                                if s >= 4 or not (first and l == 0):
                                    act.wait_ge(pv_done, g * NT + s - 3)
                                    if s >= 4:
                                        k = g * (NT - 1) + max(s - 5, 0) + 1
                                    else:
                                        k = (g - 1) * (NT - 1) + NT + s - 4
                                    if h and last and l == BODY - 1 and s >= 4:
                                        act.wait_ge(z1_done, max(s - 5, 0) + 1)
                                    else:
                                        act.wait_ge(z_done, k)
                                side = int(s - u * TC > 1)
                                nc.scalar.activation(PR[:, (2 * s + h) % RING, :], ST[h][:, :], ACT.Exp,
                                                     bias=far[:, b, h, side:side + 1]).then_inc(exp_ready, 1)
                            if s in todo and todo[s][0] != "v":
                                kind, c, n = todo[s]
                                high(kind, 1 - b, (u + 2) % NC if kind == "q" else c, n)
                            if s == 1 and u == 0 and not (last and b):
                                split_weights(p + 1, 1 - b)
                            if s == 10 and first and l < NC:
                                need(act, ctx_ready, l)
                                nc.scalar.activation(CT[1 - l % 2][:, :], sT[:, l * CH:(l + 1) * CH], ACT.Exp, scale=-1.0).then_inc(moe_exp, 1)
                loop(act, body)

            @block.vector
            def _(dve):
                links = [0, None]

                def link(ins):
                    links[0] += 1
                    ins.then_inc(chain, 1)
                    dve.wait_ge(chain, links[0] if links[1] is None else links[1] + links[0])

                def split_weights(p, b):
                    dve.wait_ge(wh_ready, p + 1)
                    nc.vector.tensor_tensor(WL[:, b, :], WR[:, :], raw(WH[:, b, :]), ALU.subtract).then_inc(wl_ready, 1)

                def table_far(p, b, h):
                    dve.wait_ge(t_loaded, (p * 2 + h + 1) * 32)
                    nc.vector.tensor_copy(far[:, b, h, 0:1], TR[:, 0, NEAR - 1:NEAR])
                    link(nc.vector.tensor_copy(far[:, b, h, 1:2], TR[:, 0, 0:1]))
                    link(nc.vector.tensor_tensor(fd[:, h:h + 1], far[:, b, h, 1:2], far[:, b, h, 0:1], ALU.subtract))
                    dve.wait_ge(c_loaded, 16)
                    nc.vector.tensor_scalar(fm[:, b, h, :, :], mask[:, :, :], fd[:, h:h + 1], far[:, b, h, 0:1],
                                            ALU.mult, ALU.add)

                def table_side(b, h, side):
                    f = far[:, b, h, side:side + 1]
                    nc.vector.tensor_scalar(TM[:, b, h, side, :], TR[:, 1, :], f, None, ALU.subtract)
                    link(nc.vector.tensor_scalar(TH[:, b, h, side, :], TR[:, 0, :], f, None, ALU.subtract))
                    last = nc.vector.scalar_tensor_tensor(out=TL[:, b, h, side, :], in0=TR[:, 0, :], scalar=f,
                                                          in1=raw(TH[:, b, h, side, :]), op0=ALU.subtract,
                                                          op1=ALU.subtract)
                    if side:
                        last.then_inc(tab_ready, 1)

                def low(kind, b, c, n, m, part, src=MP):
                    if part == 0:
                        dve.wait_ge(mp_ready, n + 1)
                    if kind == "v":
                        if part == 0:
                            nc.vector.tensor_copy(V[b][:, c * TC:(c + 1) * TC, :],
                                                  src[:, :].rearrange("p (t d) -> p t d", t=TC)).then_inc(mp_free, 1)
                        return
                    if part == 0:
                        dve.wait_ge(hi_ready, m + 1)
                    cs = slice(c * CH, (c + 1) * CH)
                    dst, hi = ((Q2[part][0:DK, cs], Q1[part]) if kind == "q" else
                               (K1[b][part][DK:P, cs], K1[b][part]))
                    ins = nc.vector.tensor_tensor(dst, src[part * DK:(part + 1) * DK, :], raw(hi[0:DK, cs]), ALU.subtract)
                    if part:
                        ins.then_inc(mp_free, 1)

                def reduce(n0, m, banks=SM):
                    h, t, c = m // (TC * NC), m // NC % TC, m % NC
                    dve.wait_ge(sm_ready, n0 + m + 1)
                    nc.vector.reduce_max(mx[:, h, t, c:c + 1], banks[m % len(banks)][:, :], AX).then_inc(mx_ready, 1)

                def combine(g, b, u):
                    dve.wait_ge(mx_ready, (g + 1) * 2 * TC * NC)
                    link(nc.vector.tensor_tensor(mxb[:, :, :, :], mx[:, :, :, :], fm[:, b, :, u * TC:(u + 1) * TC, :], ALU.add))
                    nc.vector.tensor_reduce(nm[:, :, :], mxb[:, :, :, :], AX, ALU.max, negate=True).then_inc(nm_ready, 1)

                def rows(g, u):
                    dve.wait_ge(mt_ready, g + 1)
                    for h in range(2):
                        src = MV[0:TC, h * P:(h + 1) * P].unsqueeze(1).to_broadcast([TC, TC, P])
                        dst = Q2[h][DK:DK + TC, u * CH:(u + 1) * CH].rearrange("p (t q) -> p t q", t=TC)
                        own = ident[0:TC, 0:TC].unsqueeze(2).to_broadcast([TC, TC, P])
                        last = nc.vector.tensor_tensor(dst, src, own, ALU.mult)
                    last.then_inc(rows_ready, 1)

                def invert(g, i, after_silu=False):
                    if i == 0:
                        dve.wait_ge(zb_ready, g + 1)
                        need(dve, wo_ready, g)
                        if after_silu:
                            dve.wait_ge(silu_stored, (g + 1) * 16)
                    cs = slice(i * DK, (i + 1) * DK)
                    return nc.vector.reciprocal(rz[:, cs], MV[:, cs])

                def sum_tile(s):
                    z = Z[:, 1, 1, :]
                    dve.wait_ge(exp_ready, (NUNIT - 1) * 2 * NT + 2 * s + 2)
                    if s == 1:
                        dve.wait_ge(zb_ready, NUNIT - 2)
                        a = PR[:, 1, :]
                    else:
                        dve.wait_ge(z1_done, s - 1)
                        a = z
                    nc.vector.tensor_tensor(z, a, PR[:, (2 * s + 1) % RING, :], ALU.add).then_inc(z1_done, 1)

                def gate(c):
                    cs = slice(c * CH, (c + 1) * CH)
                    if c == 0:
                        dve.wait_ge(silu_back, 16)
                    dve.wait_ge(sum_ready, NUNIT - NC + c + 1)
                    nc.vector.tensor_tensor(silu_b[:, cs], silu_b[:, cs], sT[:, cs], ALU.mult).then_inc(gated_ready, 1)

                def add_input(c):
                    dve.wait_ge(x_back, 16 * (c + 1))
                    dve.wait_ge(back_ready, c + 1)
                    nc.vector.tensor_tensor(x_b, MP[:, :].rearrange("p (t d) -> p t d", t=TC), x_b,
                                            ALU.add).then_inc(out_ready, 1)

                def silu(l, i):
                    e = CT[1 - l % 2]
                    if i == 0:
                        dve.wait_ge(moe_exp, l + 1)
                        link(nc.vector.tensor_scalar(e[:, :], e[:, :], 1.0, None, ALU.add))
                    elif i < 5:
                        cs = slice((i - 1) * P, i * P)
                        ins = nc.vector.reciprocal(e[:, cs], e[:, cs])
                        if i == 4:
                            link(ins)
                    else:
                        need(dve, wo_ready, l)
                        nc.vector.tensor_tensor(rz[:, :], e[:, :], sT[:, l * CH:(l + 1) * CH], ALU.mult).then_inc(silu_ready, 1)

                def normalise(g, par):
                    dve.wait_ge(pv_done, (g + 1) * NT)
                    nc.vector.tensor_tensor(rz[:, :], CT[par][:, :], rz[:, :], ALU.mult).then_inc(ctx_ready, 1)

                def accumulate(g, u, first_pair=False):
                    dve.wait_ge(wo_ready, g + 1)
                    cs = slice(u * CH, (u + 1) * CH)
                    if first_pair:
                        dve.wait_ge(silu_ready, u + 1)
                        nc.vector.tensor_copy(sT[:, cs], MV[:, :]).then_inc(sum_ready, 1)
                        return
                    need(dve, sum_ready, g - NC + 1)
                    nc.vector.tensor_tensor(sT[:, cs], MV[:, :], sT[:, cs], ALU.add).then_inc(sum_ready, 1)

                nc.vector.tensor_copy(identr[:, :], ident[:, :])
                nc.vector.tensor_copy(ident16[:, :], ident[:, :])

                def first_table(h):
                    table_far(0, 0, h)
                    for side in range(2):
                        table_side(0, h, side)

                for n, (kind, c) in enumerate(start_jobs[:1 + NC]):
                    for part in range(2):
                        low(kind, 0, c, n, n, part, start_banks[n % 5])
                    if n == 1:
                        first_table(0)
                for m in range(2 * TC * NC):
                    reduce(0, m, start_maxima)
                    if m == 5:
                        for part in range(2):
                            low("q", 0, 1, 1 + NC, 1 + NC, part, start_banks[0])
                    if m == 9:
                        first_table(1)
                dve.wait_ge(const_ready, 5)
                combine(0, 0, 0)
                rows(0, 0)
                start_links = links[0] + 2 * NC
                body_links = 2 * 2 * 4 + BODY * 2
                invert_at = [(3, 0), (3, 1), (3, 2), (4, 1), (4, 2), (5, 0), (5, 1), (5, 2)]
                silu_at = [(11, 1), (12, 0), (12, 2), (13, 0), (13, 1), (15, 0)]

                def body(it, first, last):
                    links[:] = [0, start_links - (2 * NC if first else 0) + it * body_links]
                    for l in range(BODY):
                        b, u = l // NC, l % NC
                        g, p = it * BODY + l, it * 2 + b
                        nb, nu = (l + 1) % BODY // NC, (l + 1) % NC
                        final, opening = last and l == BODY - 1, first and l == 0
                        todo = {slot: (kind, c, n, m) for kind, slot, c, n, m in jobs(it, l, last)}
                        before = [] if opening else jobs(it, l - 1, last) if l else jobs(it - 1, BODY - 1, False)
                        late = [(kind, c, n, m) for kind, slot, c, n, m in before if slot == NT - 1]
                        with_silu = first and l < NC
                        for s in range(NT):
                            chunks = [] if final else chunks_of(s)
                            for k in range(3):
                                for m in chunks[k:k + 1]:
                                    reduce((g + 1) * 2 * TC * NC, m)
                                if not opening:
                                    if (s, k) in invert_at:
                                        ins = invert(g - 1, invert_at.index((s, k)), first and l <= NC)
                                    if (s, k) == (6, 0):
                                        link(ins)
                                        normalise(g - 1, (l - 1) % 2)
                                    if (s, k) == (9, 1):
                                        accumulate(g - 1, (u - 1) % NC, first and l <= NC)
                                elif (s, k) == (6, 0):
                                    links[0] += 1
                                    dve.sem_inc(chain, 1)
                                if s - 1 in todo and k:
                                    kind, c, n, m = todo[s - 1]
                                    low(kind, 1 - b, (u + 2) % NC if kind == "q" else c, n, m, k - 1)
                                if s == 0 and k and late:
                                    kind, c, n, m = late[0]
                                    low(kind, 1 - (b if u else 1 - b), c, n, m, k - 1)
                                if not (last and b):
                                    if u == 0 and (s, k) == (2, 1):
                                        split_weights(p + 1, 1 - b)
                                    if u in (1, 2) and (s, k) == (7, 1):
                                        table_far(p + 1, 1 - b, u - 1)
                                    if u in (1, 2) and (s, k) in ((9, 2), (12, 1)):
                                        table_side(1 - b, u - 1, (s - 9) // 3)
                                if (s, k) == (12, 2) and not final:
                                    combine(g + 1, nb, nu)
                                if (s, k) == (14, 2) and not final:
                                    rows(g + 1, nu)
                                if final and s >= 2 and k == 2:
                                    sum_tile(s - 1)
                                if last and l > NC and (s, k) == (11, 1):
                                    gate(l - NC - 1)
                                if last and l > NC and (s, k) == (14, 0):
                                    add_input(l - NC - 1)
                                if with_silu and (s, k) in silu_at:
                                    silu(l, silu_at.index((s, k)))
                    assert last or links[0] + (0 if first else 2 * NC) == body_links + 2 * NC, (links, body_links)
                loop(dve, body)
                sum_tile(NT - 1)
                for i in range(8):
                    ins = invert(NUNIT - 1, i)
                link(ins)
                normalise(NUNIT - 1, 1)
                accumulate(NUNIT - 1, NC - 1)
                gate(NC - 1)
                add_input(NC - 1)


def build(nc, x, wq, wk, wv, wo, emb, wr, br, w1, b1, w2, b2, onehot, ident_c, mask_c, out):
    vec = nc.dram_tensor("bias_by_distance", [2, H, CH], F32, kind="Internal").ap()
    tabs = [nc.dram_tensor(f"bias_window{a}", [H, P, NEAR], F32, kind="Internal").ap() for a in range(2)]
    gates_d = nc.dram_tensor("gates", [E, S], F32, kind="Internal").ap()
    silu_d = nc.dram_tensor("silu", [D, S], F32, kind="Internal").ap()
    with ExitStack() as ctx:
        ident = ctx.enter_context(nc.sbuf_tensor("ident", [P, P], F32))
        with ExitStack() as ctx:
            xh, xl = (ctx.enter_context(nc.sbuf_tensor(n, [P, S], F32R)) for n in ("xh", "xl"))
            first_pair = [ctx.enter_context(t) for t in (
                nc.sbuf_tensor("WR", [P, 3 * P], F32), nc.sbuf_tensor("WH", [P, 2, 3 * P], F32R),
                nc.sbuf_tensor("WL", [P, 2, 3 * P], F32R), nc.semaphore("w_loaded"), nc.semaphore("wh_ready"),
                nc.semaphore("wl_ready"))]
            gates_stored, tabs_stored = (ctx.enter_context(nc.semaphore(n)) for n in ("gates_stored", "tabs_stored"))
            sT = ctx.enter_context(nc.sbuf_tensor("sT", [P, S], F32))
            with ExitStack() as until_attention:
                weights = ExpertWeights(nc, until_attention)
                g8 = until_attention.enter_context(nc.sbuf_tensor("g8", [E, S], F32))
                prepare(nc, x, emb, onehot, ident_c, wr, br, xh, xl, ident, vec, tabs, gates_d, w1, b1, w2, b2,
                        weights, g8, gates_stored, tabs_stored)
                experts(nc, w1, b1, w2, b2, xh, xl, gates_d, gates_stored, sT, wq, wk, wv, weights, first_pair)
            attention(nc, wq, wk, wv, wo, tabs, mask_c, xh, xl, ident, sT, tabs_stored, silu_d, x, out, first_pair)


_INS = ["L0_attn_hidden_states", "L0_attn_Wq", "L0_attn_Wk", "L0_attn_Wv", "L0_attn_Wo", "L0_attn_rel_bias_emb",
        "L0_ffn_Wr", "L0_ffn_br", "L0_ffn_W1", "L0_ffn_b1", "L0_ffn_W2", "L0_ffn_b2"]


def constants():
    import numpy as np
    starts = [0, 1, 2, 3, 4, 5, 6, 7, 8, 12, 16, 23, 32, 46, 64, 91]
    onehot = np.zeros((32, 2, 512), np.float32)
    for j in range(511):
        for a, rel in enumerate((255 - j, j - 255)):
            size = max(b for b in range(16) if starts[b] <= abs(rel))
            onehot[size + 16 * (rel > 0), a, j] = 1.0
    ident = np.eye(128, dtype=np.float32)
    mask = np.zeros((128, 16, 4), np.float32)
    for t in range(16):
        for c in range(4):
            mask[:, t, c] = float(t - 4 * c <= 1)
    return {"onehot": onehot, "ident": ident, "mask": mask}


def kernel(**inputs):
    import numpy as _np
    import concourse.bacc as _bacc
    from concourse import mybir as _mybir
    from concourse.bass_utils import run_bass_kernel_spmd as _run

    nc = _bacc.Bacc("TRN2", target_bir_lowering=False, num_devices=1)
    arrays, args = {}, []
    given = {n: inputs[n] for n in _INS}
    given.update(constants())
    for name, a in given.items():
        a = _np.ascontiguousarray(a)
        arrays[f"in_{name}"] = a
        args.append(nc.dram_tensor(f"in_{name}", a.shape, _mybir.dt.from_np(a.dtype), kind="ExternalInput").ap())
    args.append(nc.dram_tensor("out_0", (1, 2048, 128), _mybir.dt.float32, kind="ExternalOutput").ap())
    build(nc, *args)
    r = _run(nc, [arrays], core_ids=[0])
    return r.results[0]["out_0"]
```
